# Optimizing a Trainium2 kernel written in Bass

```python
import numpy as np
import jax
import jax.numpy as jnp

def _softmax(x, axis=-1):
    return jax.nn.softmax(x, axis=axis)

def _gelu(x):
    return jax.nn.gelu(x, approximate=True)

def _silu(x):
    return jax.nn.silu(x)

def _sigmoid(x):
    return jax.nn.sigmoid(x)

def _layernorm(x, axis=-1, eps=1e-05):
    m = jnp.mean(x, axis=axis, keepdims=True)
    v = jnp.var(x, axis=axis, keepdims=True)
    return (x - m) / jnp.sqrt(v + eps)

def _scatter_add(tgt, idx, src, axis=0):
    return tgt.at[idx].add(src)

def _segment_sum(src, seg, n):
    return jax.ops.segment_sum(src, seg, n)
kernel_name = 'mk_adaln_ffn_d1_seqx_r4_fa577a'

def setup_inputs(seed: int=0):
    np.random.seed(seed)
    _w = jnp.asarray

    def _rec_inputs():
        import jax
        import jax.numpy as jnp
        _rk = jax.random.key(seed)
        x = -8.015e-05 + 0.9999 * jax.random.normal(jax.random.fold_in(_rk, 1), (64, 64, 512), jnp.float32)
        _lenS = 64 - jax.random.randint(jax.random.fold_in(_rk, 7), (64,), 0, max(1, 64 // 4) + 1, jnp.int32)
        _lenS2 = 64 - jax.random.randint(jax.random.fold_in(_rk, 8), (64,), 0, max(1, 64 // 4) + 1, jnp.int32)
        cond_1024 = 0.00191187 + 0.999416 * jax.random.normal(jax.random.fold_in(_rk, 11), (64, 256), jnp.float32)
        return (x, cond_1024)
    x, cond_1024 = _rec_inputs()

    def _L0_cond_setup():
        import jax, jax.numpy as jnp
        import numpy as np
        B, N, V_DIM, Q_DIM = (64, 100, 512, 256)
        key = jax.random.key(seed)
        k1, k2, k3, k4 = jax.random.split(key, 4)
        v = jax.random.normal(k1, (B, N, V_DIM), dtype=jnp.float32)
        q = jax.random.normal(k2, (B, Q_DIM), dtype=jnp.float32)
        W3 = jax.random.normal(k3, (Q_DIM, V_DIM), dtype=jnp.float32) * (1.0 / np.sqrt(Q_DIM))
        b3 = jnp.zeros((V_DIM,), dtype=jnp.float32)
        W2 = jax.random.normal(k4, (V_DIM, V_DIM), dtype=jnp.float32) * (1.0 / np.sqrt(V_DIM))
        b2 = jnp.zeros((V_DIM,), dtype=jnp.float32)
        return {'v': v, 'q': q, 'W3': W3, 'b3': b3, 'W2': W2, 'b2': b2}
    _L0_cond_all = _L0_cond_setup()
    _L0_cond_in = {k: v for k, v in _L0_cond_all.items() if k in ('W3', 'b3', 'W2', 'b2')}
    del _L0_cond_all

    def _L0_ffn_setup():
        import jax, jax.numpy as jnp
        import numpy as np
        B, S, D, E, R, TOP_K = (4, 1024, 512, 6, 16, 2)
        key = jax.random.key(seed)
        ks = jax.random.split(key, 9)
        scale = 0.02
        return {'x': jax.random.normal(ks[0], (B, S, D), dtype=jnp.float32), 'W_base': jax.random.normal(ks[1], (D, D), dtype=jnp.float32) * scale, 'b_base': jax.random.normal(ks[2], (D,), dtype=jnp.float32) * scale, 'A_s': jax.random.normal(ks[3], (D, R), dtype=jnp.float32) * scale, 'B_s': jax.random.normal(ks[4], (R, D), dtype=jnp.float32) * scale, 'A_r': jax.random.normal(ks[5], (E, D, R), dtype=jnp.float32) * scale, 'B_r': jax.random.normal(ks[6], (E, R, D), dtype=jnp.float32) * scale, 'W_router': jax.random.normal(ks[7], (D, E), dtype=jnp.float32) * scale, 'b_router': jax.random.normal(ks[8], (E,), dtype=jnp.float32) * scale}
    _L0_ffn_all = _L0_ffn_setup()
    _L0_ffn_in = {k: v for k, v in _L0_ffn_all.items() if k in ('W_base', 'b_base', 'A_s', 'B_s', 'A_r', 'B_r', 'W_router', 'b_router')}
    del _L0_ffn_all
    return {'x': x, 'cond_1024': cond_1024, 'L0_cond_W3': _L0_cond_in['W3'], 'L0_cond_b3': _L0_cond_in['b3'], 'L0_cond_W2': _L0_cond_in['W2'], 'L0_cond_b2': _L0_cond_in['b2'], 'L0_ffn_W_base': _L0_ffn_in['W_base'], 'L0_ffn_b_base': _L0_ffn_in['b_base'], 'L0_ffn_A_s': _L0_ffn_in['A_s'], 'L0_ffn_B_s': _L0_ffn_in['B_s'], 'L0_ffn_A_r': _L0_ffn_in['A_r'], 'L0_ffn_B_r': _L0_ffn_in['B_r'], 'L0_ffn_W_router': _L0_ffn_in['W_router'], 'L0_ffn_b_router': _L0_ffn_in['b_router']}

def reference(x, cond_1024, L0_cond_W3, L0_cond_b3, L0_cond_W2, L0_cond_b2, L0_ffn_W_base, L0_ffn_b_base, L0_ffn_A_s, L0_ffn_B_s, L0_ffn_A_r, L0_ffn_B_r, L0_ffn_W_router, L0_ffn_b_router):
    import jax
    import jax.numpy as jnp

    def _L0_cond_ref(v, q, W3, b3, W2, b2):
        import jax, jax.numpy as jnp
        import numpy as np
        B, N, V_DIM, Q_DIM = (64, 100, 512, 256)
        q_emb = jax.nn.relu(q @ W3 + b3)
        n = v.shape[1]
        v_sum = jnp.sum(v, axis=1, keepdims=True)
        x = (n * v + v_sum) * q_emb[:, None, :]
        return jax.nn.relu(x @ W2 + b2)

    def _L0_ffn_ref(x, W_base, b_base, A_s, B_s, A_r, B_r, W_router, b_router):
        import jax, jax.numpy as jnp
        import numpy as np
        B, S, D, E, R, TOP_K = (4, 1024, 512, 6, 16, 2)
        base_out = jax.lax.stop_gradient(jnp.einsum('bsd,df->bsf', x, W_base) + b_base)
        shared_out = jnp.einsum('bsr,rf->bsf', jnp.einsum('bsd,dr->bsr', x, A_s), B_s)
        gates = jax.nn.softmax(jnp.einsum('bsd,de->bse', x, W_router) + b_router, axis=-1)
        topk_w, topk_i = jax.lax.top_k(gates, TOP_K)
        w_per_e = jnp.sum(topk_w[..., None] * jax.nn.one_hot(topk_i, E, dtype=x.dtype), axis=2)
        h = jnp.einsum('bsd,edr->bser', x, A_r)
        hw = h * w_per_e[..., None]
        routed_out = jnp.einsum('bser,erf->bsf', hw, B_r)
        return base_out + shared_out + routed_out
    x = x + _L0_ffn_ref(_L0_cond_ref(x, cond_1024, L0_cond_W3, L0_cond_b3, L0_cond_W2, L0_cond_b2), L0_ffn_W_base, L0_ffn_b_base, L0_ffn_A_s, L0_ffn_B_s, L0_ffn_A_r, L0_ffn_B_r, L0_ffn_W_router, L0_ffn_b_router)
    return x

_drawn_inputs = setup_inputs


def setup_inputs(seed=0):
    import zlib

    import numpy as np

    out = dict(_drawn_inputs(seed))
    spreads = {'L0_cond_b3': (0.0, 0.1), 'L0_cond_b2': (0.0, 2.0)}
    factors = {'L0_ffn_b_base': 42.225, 'L0_ffn_b_router': 200.0}
    for name, (base, spread) in spreads.items():
        noise = np.random.default_rng([zlib.crc32(name.encode()), seed]).standard_normal(out[name].shape)
        drawn = base * np.exp(spread * noise) if base else spread * noise
        out[name] = jnp.asarray(drawn.astype(out[name].dtype))
    for name, factor in factors.items():
        out[name] = (out[name] * factor).astype(out[name].dtype)
    return out
```

```python
import concourse.bass as bass
from concourse import mybir
from contextlib import ExitStack


def adaln_ffn(nc, x, cond, W3, b3, W2, b2, W_base, b_base, A_s, B_s, A_r, B_r, W_router, b_router, out):
    F32 = mybir.dt.float32
    F32R = mybir.dt.float32r
    ALU = mybir.AluOpType
    ACT = mybir.ActivationFunctionType
    AX = mybir.AxisListType

    P = 128
    B, N, D = x.shape
    Q = cond.shape[1]
    E, _, R = A_r.shape
    KC = D // P
    QC = Q // P
    TG = 512
    TT = TG // P
    BG = TG // N
    NG = B * N // TG
    ONE = E
    SH = 16
    RO = 32
    assert ONE < SH and SH + R <= RO and RO + E * R == P and TT == KC and NG % 2 == 0

    x_groups = x.rearrange("b n d -> (b n) d").rearrange("(g t p) d -> g p t d", t=TT, p=P)
    out_groups = out.rearrange("b n d -> (b n) d").rearrange("(g t p) d -> g p t d", t=TT, p=P)

    ctx = ExitStack()
    with ctx:
        def sb(name, shape, dt=F32):
            return ctx.enter_context(nc.sbuf_tensor(name, shape, dt))

        def bank(name):
            return ctx.enter_context(nc.psum_tensor(name, [P, 512], F32))

        def sem(name):
            return ctx.enter_context(nc.semaphore(name))

        x_nat = [sb(f"x_nat{i}", [P, TT, D]) for i in range(2)]
        out_nat = [sb(f"out_nat{i}", [P, TT, D]) for i in range(2)]
        vsum = [sb(f"vsum{i}", [P, BG]) for i in range(2)]
        x1_sum = [sb(f"x1_sum{i}", [P, TG]) for i in range(2)]
        x1_full = [sb(f"x1_full{i}", [P, TG]) for i in range(2)]
        x1_hi = [sb(f"x1_hi{i}", [P, KC, TG], F32R) for i in range(2)]
        x1_lo = [sb(f"x1_lo{i}", [P, KC, TG], F32R) for i in range(2)]
        y_full = [sb(f"y_full{i}", [P, TG]) for i in range(2)]
        y_hi = sb("y_hi", [P, KC, TG], F32R)
        y_lo = sb("y_lo", [P, KC, TG], F32R)
        h_sb = sb("h_sb", [P, TG])
        hw_full = sb("hw_full", [P, TG])
        hw_hi = sb("hw_hi", [P, TG], F32R)
        hw_lo = sb("hw_lo", [P, TG], F32R)

        W2_f = sb("W2_f", [P, KC, D])
        Wb_f = sb("Wb_f", [P, KC, D])
        Wd_f = sb("Wd_f", [P, KC, P])
        Wu_f = sb("Wu_f", [P, D])
        W2_hi = sb("W2_hi", [P, KC, D], F32R)
        W2_lo = sb("W2_lo", [P, KC, D], F32R)
        Wb_hi = sb("Wb_hi", [P, KC, D], F32R)
        Wb_lo = sb("Wb_lo", [P, KC, D], F32R)
        Wd_hi = sb("Wd_hi", [P, KC, P], F32R)
        Wd_lo = sb("Wd_lo", [P, KC, P], F32R)
        Wu_hi = sb("Wu_hi", [P, D], F32R)
        Wu_lo = sb("Wu_lo", [P, D], F32R)
        W3_sb = sb("W3_sb", [P, QC, D])
        cond_sb = sb("cond_sb", [B, Q])
        condT = sb("condT", [P, QC, B])
        qT = sb("qT", [P, KC, B])
        b3_sb = sb("b3_sb", [P, KC])
        b2_sb = sb("b2_sb", [P, KC])
        h_bias = sb("h_bias", [P, 1])
        ident = sb("ident", [P, P])
        earlier = sb("earlier", [P, E, E])

        lmax = sb("lmax", [P, TT])
        logit = sb("logit", [P, TT, E])
        diff = sb("diff", [P, TT, E, E])
        tie = sb("tie", [P, TT, E, E])
        beats = sb("beats", [P, TT, E, E])
        rank = sb("rank", [P, TT, E])
        expo = sb("expo", [P, TT, E])
        expo_top = sb("expo_top", [P, TT, E])
        den = sb("den", [P, TT])
        rden = sb("rden", [P, TT])
        w_nat = sb("w_nat", [P, TT, P])

        prod = [bank(f"prod{i}") for i in range(4)]
        xT = [bank(f"xT{i}") for i in range(2)]
        hT = bank("hT")
        gate_ps = bank("gate_ps")
        h_nat = gate_ps[:, :].rearrange("p (t r) -> p t r", r=P)
        gate_logits = h_nat[:, :, 0:E]

        x_loaded = [sem(f"x_loaded{i}") for i in range(2)]
        stored = [sem(f"stored{i}") for i in range(2)]
        cond_loaded, W3_loaded, b3_loaded, b2_loaded = sem("cond_loaded"), sem("W3_loaded"), sem("b3_loaded"), sem("b2_loaded")
        W2_loaded, Wb_loaded, Wd_loaded, Wu_loaded = sem("W2_loaded"), sem("Wb_loaded"), sem("Wd_loaded"), sem("Wu_loaded")
        bias_loaded = sem("bias_loaded")
        zeroed, ident_ready, const_ready = sem("zeroed"), sem("ident_ready"), sem("const_ready")
        bias_ready = sem("bias_ready")
        condT_done, condT_copied, q_done, qT_ready = sem("condT_done"), sem("condT_copied"), sem("q_done"), sem("qT_ready")
        W_hi_ready, W_lo_ready = sem("W_hi_ready"), sem("W_lo_ready")
        xT_done, vsum_ready, x1_sum_ready, x1_full_ready = sem("xT_done"), sem("vsum_ready"), sem("x1_sum_ready"), sem("x1_full_ready")
        x1_hi_ready, x1_lo_ready = sem("x1_hi_ready"), sem("x1_lo_ready")
        m1_done, y_full_ready, y_hi_ready, y_lo_ready = sem("m1_done"), sem("y_full_ready"), sem("y_hi_ready"), sem("y_lo_ready")
        h_done, h_ready = sem("h_done"), sem("h_ready")
        logits_done, logit_ready, expo_ready, gate_step = sem("logits_done"), sem("logit_ready"), sem("expo_ready"), sem("gate_step")
        w_ready, wT_done = sem("w_ready"), sem("wT_done")
        hw_ready, hw_hi_ready, hw_lo_ready = sem("hw_ready"), sem("hw_hi_ready"), sem("hw_lo_ready")
        m2_done, out_ready = sem("m2_done"), sem("out_ready")

        NW2, NWB = KC, 2 * KC
        NWD, NWU = 2 * KC + 1, 2 * KC + 2
        GATE_STEPS = 8

        block = ctx.enter_context(nc.Block())

        def per_batch(ap):
            return ap.rearrange("p (b n) -> p b n", n=N)


        def steps(eng, step):
            step(0, 0, first=True, last=False)
            with eng.Fori(0, (NG - 2) // 2) as pair:
                for half in range(2):
                    step(pair * 2 + (1 + half), (1 + half) % 2, first=False, last=False)
            step(NG - 1, (NG - 1) % 2, first=False, last=True)

        @block.sync
        def _(sp):
            sp.dma_start(cond_sb[:, :], cond).then_inc(cond_loaded, 16)
            sp.dma_start(W3_sb[:, :, :], W3.rearrange("(k p) d -> p k d", p=P)).then_inc(W3_loaded, 16)
            sp.dma_start(x_nat[0][:, :, :], x_groups[0]).then_inc(x_loaded[0], 16)
            sp.dma_start(W2_f[:, :, :], W2.rearrange("(k p) d -> p k d", p=P)).then_inc(W2_loaded, 16)
            sp.dma_start(x_nat[1][:, :, :], x_groups[1]).then_inc(x_loaded[1], 16)
            sp.dma_start(Wb_f[:, :, :], W_base.rearrange("(k p) d -> p k d", p=P)).then_inc(Wb_loaded, 16)

            def step(g, par, load):
                for t in range(TT):
                    sp.wait_ge(out_ready, TT * g + t + 1)
                    sp.dma_start(out_groups[g, :, t, :] if isinstance(g, int) else
                                 out_groups[bass.ds(g, 1), :, t, :].rearrange("a p d -> (a p) d"),
                                 out_nat[par][:, t, :]).then_inc(stored[par], 16)
                if load:
                    sp.dma_start(x_nat[par][:, :, :],
                                 x_groups[g + 2] if isinstance(g, int) else
                                 x_groups[bass.ds(g + 2, 1)].rearrange("a p t d -> (a p) t d")).then_inc(x_loaded[par], 16)

            step(0, 0, True)
            with sp.Fori(0, (NG - 4) // 2) as pair:
                for half in range(2):
                    step(pair * 2 + (1 + half), (1 + half) % 2, True)
            for g in range(NG - 3, NG):
                step(g, g % 2, g + 2 < NG)
            for par in range(2):
                sp.wait_ge(stored[par], 16 * TT * (NG // 2))

        @block.gpsimd
        def _(pool):
            nc.gpsimd.memset(ident[:, :], 0.0).then_inc(zeroed, 1)
            nc.gpsimd.memset(earlier[:, :, :], 1.0).then_inc(zeroed, 1)
            nc.gpsimd.memset(Wd_f[:, :, :], 0.0).then_inc(zeroed, 1)
            nc.gpsimd.memset(Wu_f[:, :], 0.0).then_inc(zeroed, 1)
            pool.wait_ge(zeroed, 2)
            nc.gpsimd.affine_select(out=ident[:, :], in_=ident[:, :], compare_op=ALU.not_equal, fill=1.0,
                                    base=0, pattern=[[-1, P]], channel_multiplier=1).then_inc(ident_ready, 1)
            nc.gpsimd.affine_select(out=earlier[:, :, :], in_=earlier[:, :, :], compare_op=ALU.is_gt, fill=0.0,
                                    base=0, pattern=[[1, E], [-1, E]], channel_multiplier=0).then_inc(const_ready, 1)
            nc.gpsimd.memset(w_nat[:, :, 0:RO], 0.0).then_inc(zeroed, 1)
            pool.wait_ge(zeroed, 5)
            nc.gpsimd.memset(w_nat[:, :, ONE:ONE + 1], 1.0).then_inc(const_ready, 1)
            nc.gpsimd.memset(w_nat[:, :, SH:SH + R], 1.0).then_inc(const_ready, 1)

            def scale(g, c):
                n = KC * g + c
                pool.wait_ge(x1_sum_ready, n + 1)
                if not (isinstance(g, int) and n < 2):
                    pool.wait_ge(x1_lo_ready, n - 1)
                nc.gpsimd.tensor_tensor(per_batch(x1_full[c % 2][:, :]), per_batch(x1_sum[c % 2][:, :]),
                                        qT[:, c, bass.ds(BG * g, BG)].unsqueeze(2).to_broadcast([P, BG, N]),
                                        ALU.mult).then_inc(x1_full_ready, 1)

            pool.wait_ge(qT_ready, KC)
            for c in range(KC):
                scale(0, c)
            for c in range(KC):
                scale(1, c)
            with pool.Fori(2, NG) as g:
                for c in range(KC):
                    scale(g, c)

        @block.scalar
        def _(act):
            act.dma_start(b3_sb[:, :], b3.rearrange("(k p) -> p k", p=P), allow_slow_non_contiguous=True).then_inc(b3_loaded, 16)
            act.dma_start(b2_sb[:, :], b2.rearrange("(k p) -> p k", p=P), allow_slow_non_contiguous=True).then_inc(b2_loaded, 16)
            act.wait_ge(zeroed, 4)
            act.dma_start(Wd_f[:, :, 0:E], W_router.rearrange("(k p) e -> p k e", p=P)).then_inc(Wd_loaded, 16)
            act.dma_start(Wd_f[:, :, SH:SH + R], A_s.rearrange("(k p) r -> p k r", p=P)).then_inc(Wd_loaded, 16)
            for e in range(E):
                act.dma_start(Wd_f[:, :, RO + R * e:RO + R * (e + 1)],
                              A_r[e].rearrange("(k p) r -> p k r", p=P)).then_inc(Wd_loaded, 16)
            act.dma_start(Wu_f[ONE:ONE + 1, :], b_base.rearrange("(a d) -> a d", a=1)).then_inc(Wu_loaded, 16)
            act.dma_start(Wu_f[SH:SH + R, :], B_s).then_inc(Wu_loaded, 16)
            act.dma_start(Wu_f[RO:P, :], B_r.rearrange("e r d -> (e r) d")).then_inc(Wu_loaded, 16)
            act.wait_ge(ident_ready, 1)
            nc.scalar.activation(h_bias[:, :], ident[:, ONE:ONE + 1], ACT.Copy).then_inc(bias_ready, 1)
            act.wait_ge(bias_ready, 1)
            act.dma_start(h_bias[0:E, :], b_router.rearrange("(e a) -> e a", a=1)).then_inc(bias_loaded, 16)

            act.wait_ge(condT_done, 1)
            nc.scalar.activation(condT[:, :, :], hT[:, 0:QC * B].rearrange("p (k b) -> p k b", b=B),
                                 ACT.Copy).then_inc(condT_copied, 1)
            act.wait_ge(b3_loaded, 16)
            act.wait_ge(q_done, 1)
            for c in range(KC):
                nc.scalar.activation(qT[:, c, :], gate_ps[:, c * B:(c + 1) * B], ACT.Relu,
                                     bias=b3_sb[:, c:c + 1]).then_inc(qT_ready, 1)

            def x1_split(g, par, c):
                act.wait_ge(x1_full_ready, KC * g + c + 1)
                nc.scalar.activation(x1_hi[par][:, c, :], x1_full[c % 2][:, :], ACT.Copy).then_inc(x1_hi_ready, 1)

            def relu(g, m, first):
                n = KC * g + m
                act.wait_ge(m1_done, n + 1)
                if not (first and m < 2):
                    act.wait_ge(y_lo_ready, n - 1)
                nc.scalar.activation(y_full[m % 2][:, :], prod[m][:, :], ACT.Relu,
                                     bias=b2_sb[:, m:m + 1]).then_inc(y_full_ready, 1)
                nc.scalar.activation(y_hi[:, m, :], prod[m][:, :], ACT.Relu,
                                     bias=b2_sb[:, m:m + 1]).then_inc(y_hi_ready, 1)

            act.wait_ge(W2_loaded, 16)
            for k in range(KC):
                nc.scalar.activation(W2_hi[:, k, :], W2_f[:, k, :], ACT.Copy).then_inc(W_hi_ready, 1)
            for c in range(KC):
                x1_split(0, 0, c)
            act.wait_ge(Wb_loaded, 16)
            for k in range(KC):
                nc.scalar.activation(Wb_hi[:, k, :], Wb_f[:, k, :], ACT.Copy).then_inc(W_hi_ready, 1)
            act.wait_ge(Wd_loaded, 16 * (2 + E))
            nc.scalar.activation(Wd_hi[:, :, :], Wd_f[:, :, :], ACT.Copy).then_inc(W_hi_ready, 1)
            act.wait_ge(Wu_loaded, 48)
            nc.scalar.activation(Wu_hi[:, :], Wu_f[:, :], ACT.Copy).then_inc(W_hi_ready, 1)
            act.wait_ge(b2_loaded, 16)
            act.wait_ge(bias_loaded, 16)

            def step(g, par, first, last):
                for m in range(KC):
                    relu(g, m, first)
                if not last:
                    x1_split(g + 1, 1 - par, 0)
                act.wait_ge(h_done, g + 1)
                if not first:
                    act.wait_ge(hw_ready, g)
                nc.scalar.activation(h_sb[:, :], hT[:, :], ACT.Identity, bias=h_bias[:, 0:1]).then_inc(h_ready, 1)
                if not last:
                    x1_split(g + 1, 1 - par, 1)
                act.wait_ge(logit_ready, g + 1)
                nc.scalar.activation(expo[:, :, :], logit[:, :, :], ACT.Exp).then_inc(expo_ready, 1)
                if not last:
                    x1_split(g + 1, 1 - par, 2)
                    x1_split(g + 1, 1 - par, 3)
                act.wait_ge(hw_ready, g + 1)
                nc.scalar.activation(hw_hi[:, :], hw_full[:, :], ACT.Copy).then_inc(hw_hi_ready, 1)

            steps(act, step)

        @block.vector
        def _(dve):
            def x1_sums(g, c, first=False):
                n = KC * g + c
                dve.wait_ge(xT_done, n + 1)
                nc.vector.tensor_reduce(vsum[c % 2][:, :], per_batch(xT[c % 2][:, :]), AX.X,
                                        ALU.add).then_inc(vsum_ready, 1)
                dve.wait_ge(vsum_ready, n + 1)
                if not (first and c < 2):
                    dve.wait_ge(x1_full_ready, n - 1)
                nc.vector.scalar_tensor_tensor(
                    out=per_batch(x1_sum[c % 2][:, :]), in0=per_batch(xT[c % 2][:, :]), scalar=float(N),
                    in1=vsum[c % 2][:, :].unsqueeze(2).to_broadcast([P, BG, N]),
                    op0=ALU.mult, op1=ALU.add).then_inc(x1_sum_ready, 1)

            def x1_rest(g, par, c):
                dve.wait_ge(x1_hi_ready, KC * g + c + 1)
                nc.vector.tensor_tensor(x1_lo[par][:, c, :], x1_full[c % 2][:, :],
                                        x1_hi[par][:, c, :].bitcast(F32), ALU.subtract).then_inc(x1_lo_ready, 1)

            def y_rest(g, m):
                dve.wait_ge(y_hi_ready, KC * g + m + 1)
                nc.vector.tensor_tensor(y_lo[:, m, :], y_full[m % 2][:, :],
                                        y_hi[:, m, :].bitcast(F32), ALU.subtract).then_inc(y_lo_ready, 1)

            def W_rest(lo, full, hi, n):
                dve.wait_ge(W_hi_ready, n)
                nc.vector.tensor_tensor(lo, full, hi.bitcast(F32), ALU.subtract).then_inc(W_lo_ready, 1)

            for c in range(KC):
                x1_sums(0, c, first=True)
                W_rest(W2_lo[:, c, :], W2_f[:, c, :], W2_hi[:, c, :], c + 1)
                x1_rest(0, 0, c)
            for k in range(KC):
                W_rest(Wb_lo[:, k, :], Wb_f[:, k, :], Wb_hi[:, k, :], NW2 + k + 1)
            W_rest(Wd_lo[:, :, :], Wd_f[:, :, :], Wd_hi[:, :, :], NWD)
            W_rest(Wu_lo[:, :], Wu_f[:, :], Wu_hi[:, :], NWU)
            dve.wait_ge(const_ready, 3)

            def rank_experts(g):
                done = GATE_STEPS * g
                dve.wait_ge(logits_done, g + 1)
                nc.vector.tensor_reduce(lmax[:, :], gate_logits, AX.X, ALU.max).then_inc(gate_step, 1)
                dve.wait_ge(gate_step, done + 1)
                nc.vector.tensor_tensor(logit[:, :, :], gate_logits,
                                        lmax[:, :].unsqueeze(2).to_broadcast([P, TT, E]),
                                        ALU.subtract).then_inc(logit_ready, 1)
                dve.wait_ge(logit_ready, g + 1)
                nc.vector.tensor_tensor(diff[:, :, :, :],
                                        logit[:, :, :].unsqueeze(2).to_broadcast([P, TT, E, E]),
                                        logit[:, :, :].unsqueeze(3).to_broadcast([P, TT, E, E]),
                                        ALU.subtract).then_inc(gate_step, 1)
                dve.wait_ge(gate_step, done + 2)
                flat = "p t e j -> p t (e j)"
                nc.vector.scalar_tensor_tensor(
                    out=tie[:, :, :, :].rearrange(flat), in0=diff[:, :, :, :].rearrange(flat), scalar=0.0,
                    in1=earlier[:, :, :].rearrange("p e j -> p (e j)").unsqueeze(1).to_broadcast([P, TT, E * E]),
                    op0=ALU.is_ge, op1=ALU.mult).then_inc(gate_step, 1)
                dve.wait_ge(gate_step, done + 3)
                nc.vector.scalar_tensor_tensor(
                    out=beats[:, :, :, :].rearrange(flat), in0=diff[:, :, :, :].rearrange(flat), scalar=0.0,
                    in1=tie[:, :, :, :].rearrange(flat), op0=ALU.is_gt, op1=ALU.max).then_inc(gate_step, 1)
                dve.wait_ge(gate_step, done + 4)
                nc.vector.tensor_reduce(rank[:, :, :], beats[:, :, :, :], AX.X, ALU.add).then_inc(gate_step, 1)

            def gates(g, first):
                done = GATE_STEPS * g
                dve.wait_ge(expo_ready, g + 1)
                nc.vector.tensor_reduce(den[:, :], expo[:, :, :], AX.X, ALU.add).then_inc(gate_step, 1)
                dve.wait_ge(gate_step, done + 6)
                nc.vector.scalar_tensor_tensor(out=expo_top[:, :, :], in0=rank[:, :, :], scalar=1.5,
                                               in1=expo[:, :, :], op0=ALU.is_lt, op1=ALU.mult).then_inc(gate_step, 1)
                nc.vector.reciprocal(rden[:, :], den[:, :]).then_inc(gate_step, 1)
                dve.wait_ge(gate_step, done + 8)
                if not first:
                    dve.wait_ge(wT_done, g)
                nc.vector.tensor_tensor(w_nat[:, :, RO:P].rearrange("p t (e r) -> p t e r", r=R),
                                        expo_top[:, :, :].unsqueeze(3).to_broadcast([P, TT, E, R]),
                                        rden[:, :].unsqueeze(2).unsqueeze(3).to_broadcast([P, TT, E, R]),
                                        ALU.mult).then_inc(w_ready, 1)

            def step(g, par, first, last):
                for m in range(3):
                    y_rest(g, m)
                if not last:
                    x1_sums(g + 1, 0)
                y_rest(g, 3)
                if not last:
                    x1_sums(g + 1, 1)
                    x1_rest(g + 1, 1 - par, 0)
                rank_experts(g)
                if not last:
                    x1_sums(g + 1, 2)
                    x1_rest(g + 1, 1 - par, 1)
                gates(g, first)
                if not last:
                    x1_sums(g + 1, 3)
                    x1_rest(g + 1, 1 - par, 2)
                    x1_rest(g + 1, 1 - par, 3)
                dve.wait_ge(wT_done, g + 1)
                if not first:
                    dve.wait_ge(hw_hi_ready, g)
                nc.vector.tensor_tensor(hw_full[:, :], h_sb[:, :], gate_ps[:, :], ALU.mult).then_inc(hw_ready, 1)
                dve.wait_ge(hw_hi_ready, g + 1)
                nc.vector.tensor_tensor(hw_lo[:, :], hw_full[:, :], hw_hi[:, :].bitcast(F32),
                                        ALU.subtract).then_inc(hw_lo_ready, 1)
                if not first:
                    if isinstance(g, int):
                        dve.wait_ge(stored[par], 16 * TT * (g // 2))
                    elif par == 0:
                        dve.wait_ge(stored[par], 8 * TT * g)
                    else:
                        dve.wait_ge(stored[par], 8 * TT * (g - 1))
                for t in range(TT):
                    dve.wait_ge(m2_done, TT * g + t + 1)
                    nc.vector.tensor_tensor(out_nat[par][:, t, :], prod[t][:, :], x_nat[par][:, t, :],
                                            ALU.add).then_inc(out_ready, 1)

            steps_dve = step
            steps_dve(0, 0, first=True, last=False)
            def later(eng):
                with eng.Fori(0, (NG - 4) // 2) as pair:
                    for half in range(2):
                        steps_dve(pair * 2 + (2 + half), half % 2, first=False, last=False)
            def step1():
                steps_dve(1, 1, first=False, last=False)
            step1()
            later(dve)
            for g in range(NG - 2, NG):
                steps_dve(g, g % 2, first=False, last=g == NG - 1)

        @block.tensor
        def _(pe):
            pe.wait_ge(ident_ready, 1)
            pe.wait_ge(cond_loaded, 16)
            for k in range(QC):
                last = nc.tensor.transpose(hT[:, k * B:(k + 1) * B], cond_sb[:, k * P:(k + 1) * P], ident[0:B, 0:B])
            last.then_inc(condT_done, 1)

            def transpose_x(g, par, c, first=False):
                if c == 0:
                    if isinstance(g, int):
                        pe.wait_ge(x_loaded[par], 16 * (g // 2 + 1))
                    elif par == 0:
                        pe.wait_ge(x_loaded[par], 8 * g + 16)
                    else:
                        pe.wait_ge(x_loaded[par], 8 * g + 8)
                if not (first and c < 2):
                    pe.wait_ge(x1_sum_ready, KC * g + c - 1)
                for t in range(TT):
                    mm = nc.tensor.transpose(xT[c % 2][:, t * P:(t + 1) * P],
                                             x_nat[par][:, t, c * P:(c + 1) * P], ident[:, :])
                mm.then_inc(xT_done, 1)

            def product(psum, terms, start, stop):
                for i, (lhsT, rhs) in enumerate(terms):
                    mm = nc.tensor.matmul(psum, lhsT, rhs, start=start and i == 0,
                                          stop=stop and i == len(terms) - 1)
                return mm

            def m1(g, par, m, first):
                cols = slice(m * P, (m + 1) * P)
                if not first:
                    pe.wait_ge(out_ready, TT * (g - 1) + m + 1)
                for k in range(KC):
                    if m == 0:
                        pe.wait_ge(x1_lo_ready, KC * g + k + 1)
                    if first:
                        pe.wait_ge(W_lo_ready, k + 1)
                    mm = product(prod[m][:, :], [(W2_hi[:, k, cols], x1_hi[par][:, k, :]),
                                                 (W2_hi[:, k, cols], x1_lo[par][:, k, :]),
                                                 (W2_lo[:, k, cols], x1_hi[par][:, k, :])], k == 0, k == KC - 1)
                mm.then_inc(m1_done, 1)

            def h(g, first):
                if first:
                    pe.wait_ge(W_lo_ready, NWU)
                else:
                    pe.wait_ge(h_ready, g)
                for k in range(KC):
                    pe.wait_ge(y_lo_ready, KC * g + k + 1)
                    mm = product(hT[:, :], [(Wd_hi[:, k, :], y_hi[:, k, :]),
                                            (Wd_hi[:, k, :], y_lo[:, k, :]),
                                            (Wd_lo[:, k, :], y_hi[:, k, :])], k == 0, k == KC - 1)
                mm.then_inc(h_done, 1)

            def m2(g, t):
                toks = slice(t * P, (t + 1) * P)
                for k in range(KC):
                    product(prod[t][:, :], [(y_hi[:, k, toks], Wb_hi[:, k, :]),
                                            (y_hi[:, k, toks], Wb_lo[:, k, :]),
                                            (y_lo[:, k, toks], Wb_hi[:, k, :])], k == 0, False)

            def up(t):
                toks = slice(t * P, (t + 1) * P)
                product(prod[t][:, :], [(hw_hi[:, toks], Wu_hi[:, :]),
                                        (hw_hi[:, toks], Wu_lo[:, :]),
                                        (hw_lo[:, toks], Wu_hi[:, :])], False, True).then_inc(m2_done, 1)

            pe.wait_ge(W3_loaded, 16)
            pe.wait_ge(condT_copied, 1)
            for c in range(KC):
                for k in range(QC):
                    last = nc.tensor.matmul(gate_ps[:, c * B:(c + 1) * B], W3_sb[:, k, c * P:(c + 1) * P],
                                            condT[:, k, :], start=(k == 0), stop=(k == QC - 1))
            last.then_inc(q_done, 1)
            for c in range(KC):
                transpose_x(0, 0, c, first=True)

            def step(g, par, first, last):
                for m in range(KC):
                    m1(g, par, m, first)
                    if not last and m >= 2:
                        transpose_x(g + 1, 1 - par, m - 2)
                h(g, first)
                m2(g, 0)
                pe.wait_ge(h_ready, g + 1)
                if not first:
                    pe.wait_ge(hw_ready, g)
                for t in range(TT):
                    mm = nc.tensor.transpose(h_nat[:, t, :], h_sb[:, t * P:(t + 1) * P], ident[:, :])
                mm.then_inc(logits_done, 1)
                if not last:
                    transpose_x(g + 1, 1 - par, 2)
                m2(g, 1)
                if not last:
                    transpose_x(g + 1, 1 - par, 3)
                m2(g, 2)
                pe.wait_ge(w_ready, g + 1)
                for t in range(TT):
                    mm = nc.tensor.transpose(gate_ps[:, t * P:(t + 1) * P], w_nat[:, t, :], ident[:, :])
                mm.then_inc(wT_done, 1)
                m2(g, 3)
                pe.wait_ge(hw_lo_ready, g + 1)
                for t in range(TT):
                    up(t)

            steps(pe, step)


_INS = ['x', 'cond_1024', 'L0_cond_W3', 'L0_cond_b3', 'L0_cond_W2', 'L0_cond_b2', 'L0_ffn_W_base', 'L0_ffn_b_base',
        'L0_ffn_A_s', 'L0_ffn_B_s', 'L0_ffn_A_r', 'L0_ffn_B_r', 'L0_ffn_W_router', 'L0_ffn_b_router']
_OUTS = [((64, 64, 512), 'float32')]


def kernel(**inputs):
    import numpy as _np
    import concourse.bacc as _bacc
    from concourse import mybir as _mybir
    from concourse.bass_utils import run_bass_kernel_spmd as _run

    nc = _bacc.Bacc("TRN2", target_bir_lowering=False, num_devices=1)
    arrays, args = {}, []
    for name in _INS:
        a = _np.ascontiguousarray(inputs[name])
        arrays[f"in_{name}_dram"] = a
        args.append(nc.dram_tensor(f"in_{name}_dram", a.shape, _mybir.dt.from_np(a.dtype), kind="ExternalInput").ap())
    for i, (shape, dtype) in enumerate(_OUTS):
        dt = _mybir.dt.from_np(_np.dtype(dtype))
        args.append(nc.dram_tensor(f"out_{i}_dram", shape, dt, kind="ExternalOutput").ap())
    adaln_ffn(nc, *args)
    r = _run(nc, [arrays], core_ids=[0])
    return r.results[0]["out_0_dram"]
```

```python
import concourse.bass as bass
from concourse import mybir
from contextlib import ExitStack


def adaln_ffn(nc, x, cond, W3, b3, W2, b2, W_base, b_base, A_s, B_s, A_r, B_r, W_router, b_router, out):
    F32 = mybir.dt.float32
    F32R = mybir.dt.float32r
    ALU = mybir.AluOpType
    ACT = mybir.ActivationFunctionType
    AX = mybir.AxisListType

    P = 128
    B, N, D = x.shape
    Q = cond.shape[1]
    E, _, R = A_r.shape
    KC = D // P
    QC = Q // P
    TG = 512
    TT = TG // P
    BG = TG // N
    NG = B * N // TG
    S = 32
    NQ = P // S
    ONE = E
    SH = 16
    RO = 32
    assert ONE < SH and SH + R <= RO and RO + E * R == P and TT == KC and NG % 2 == 0

    x_groups = x.rearrange("b n d -> (b n) d").rearrange("(g t p) d -> g p t d", t=TT, p=P)
    x_quarters = x.rearrange("b n d -> (b n) d").rearrange("(g b i) (q f) -> g q i b f", b=TG // S, i=S, q=NQ)
    out_groups = out.rearrange("b n d -> (b n) d").rearrange("(g t p) d -> g p t d", t=TT, p=P)

    ctx = ExitStack()
    with ctx:
        def sb(name, shape, dt=F32):
            return ctx.enter_context(nc.sbuf_tensor(name, shape, dt))

        def bank(name):
            return ctx.enter_context(nc.psum_tensor(name, [P, 512], F32))

        def sem(name):
            return ctx.enter_context(nc.semaphore(name))

        x_nat = [sb(f"x_nat{i}", [P, TT, D]) for i in range(2)]
        x_quart = [sb(f"x_quart{i}", [P, TG // S, KC * S]) for i in range(2)]
        xT = [sb(f"xT{i}", [P, TG]) for i in range(2)]
        out_nat = [sb(f"out_nat{i}", [P, TT, D]) for i in range(2)]
        vsum = [sb(f"vsum{i}", [P, BG]) for i in range(2)]
        x1_sum = sb("x1_sum", [P, KC, TG])
        x1_full = sb("x1_full", [P, KC, TG])
        x1_hi = [sb(f"x1_hi{i}", [P, KC, TG], F32R) for i in range(2)]
        x1_lo = [sb(f"x1_lo{i}", [P, KC, TG], F32R) for i in range(2)]
        y_full = [sb(f"y_full{i}", [P, TG]) for i in range(2)]
        y_hi = sb("y_hi", [P, KC, TG], F32R)
        y_lo = sb("y_lo", [P, KC, TG], F32R)
        h_sb = sb("h_sb", [P, TG])
        h_head = sb("h_head", [P, P])
        h_nat = sb("h_nat", [P, TT, S])
        gate_logits = h_nat[:, :, 0:E]
        hw_full = sb("hw_full", [P, TG])
        hw_hi = sb("hw_hi", [P, TG], F32R)
        hw_lo = sb("hw_lo", [P, TG], F32R)

        W2_f = sb("W2_f", [P, KC, D])
        Wb_f = sb("Wb_f", [P, KC, D])
        Wd_f = sb("Wd_f", [P, KC, P])
        Wu_f = sb("Wu_f", [P, D])
        W2_hi = sb("W2_hi", [P, KC, D], F32R)
        W2_lo = sb("W2_lo", [P, KC, D], F32R)
        Wb_hi = sb("Wb_hi", [P, KC, D], F32R)
        Wb_lo = sb("Wb_lo", [P, KC, D], F32R)
        Wd_hi = sb("Wd_hi", [P, KC, P], F32R)
        Wd_lo = sb("Wd_lo", [P, KC, P], F32R)
        Wu_hi = sb("Wu_hi", [P, D], F32R)
        Wu_lo = sb("Wu_lo", [P, D], F32R)
        W3_sb = sb("W3_sb", [P, QC, D])
        cond_sb = sb("cond_sb", [B, Q])
        condT = sb("condT", [P, QC, B])
        qT = sb("qT", [P, KC, B])
        b3_sb = sb("b3_sb", [P, KC])
        b2_sb = sb("b2_sb", [P, KC])
        h_bias = sb("h_bias", [P, 1])
        ident = sb("ident", [P, P])
        earlier = sb("earlier", [P, E, E])

        lmax = sb("lmax", [P, TT])
        logit = sb("logit", [P, TT, E])
        diff = sb("diff", [P, TT, E, E])
        tie = sb("tie", [P, TT, E, E])
        beats = sb("beats", [P, TT, E, E])
        rank = sb("rank", [P, TT, E])
        expo = sb("expo", [P, TT, E])
        expo_top = sb("expo_top", [P, TT, E])
        den = sb("den", [P, TT])
        rden = sb("rden", [P, TT])
        w_nat = sb("w_nat", [P, TT, P])

        prod = [bank(f"prod{i}") for i in range(4)]
        hT = bank("hT")
        gate_ps = bank("gate_ps")

        x_loaded = [sem(f"x_loaded{i}") for i in range(2)]
        quart_loaded = [sem(f"quart_loaded{i}") for i in range(2)]
        stored = [sem(f"stored{i}") for i in range(2)]
        cond_loaded, W3_loaded, b3_loaded, b2_loaded = sem("cond_loaded"), sem("W3_loaded"), sem("b3_loaded"), sem("b2_loaded")
        W2_loaded = [sem(f"W2_loaded{c}") for c in range(KC)]
        Wb_loaded, Wd_loaded, Wu_loaded = sem("Wb_loaded"), sem("Wd_loaded"), sem("Wu_loaded")
        bias_loaded = sem("bias_loaded")
        zeroed, ident_ready, const_ready = sem("zeroed"), sem("ident_ready"), sem("const_ready")
        bias_ready = sem("bias_ready")
        condT_done, condT_copied, q_done, qT_ready = sem("condT_done"), sem("condT_copied"), sem("q_done"), sem("qT_ready")
        W_hi_ready = sem("W_hi_ready")
        W2_lo_ready, Wb_lo_ready, Wd_lo_ready, Wu_lo_ready = sem("W2_lo_ready"), sem("Wb_lo_ready"), sem("Wd_lo_ready"), sem("Wu_lo_ready")
        xT_ready, vsum_ready, x1_sum_ready, x1_full_ready = sem("xT_ready"), sem("vsum_ready"), sem("x1_sum_ready"), sem("x1_full_ready")
        x1_hi_ready, x1_lo_ready = sem("x1_hi_ready"), sem("x1_lo_ready")
        m1_done, y_full_ready, y_hi_ready, y_lo_ready = sem("m1_done"), sem("y_full_ready"), sem("y_hi_ready"), sem("y_lo_ready")
        h_done, h_ready = sem("h_done"), sem("h_ready")
        h_head_ready, logit_ready, expo_ready, gate_step = sem("h_head_ready"), sem("logit_ready"), sem("expo_ready"), sem("gate_step")
        w_ready, wT_done = sem("w_ready"), sem("wT_done")
        hw_ready, hw_hi_ready, hw_lo_ready = sem("hw_ready"), sem("hw_hi_ready"), sem("hw_lo_ready")
        m2_done, out_ready = sem("m2_done"), sem("out_ready")

        GATE_STEPS = 9

        block = ctx.enter_context(nc.Block())

        def per_batch(ap):
            return ap.rearrange("p (b n) -> p b n", n=N)


        def nth(g, par, unit):
            return (g - par) * (unit // 2) + unit

        def steps(eng, step):
            step(0, 0, first=True, last=False)
            with eng.Fori(0, (NG - 2) // 2) as pair:
                for half in range(2):
                    step(pair * 2 + (1 + half), (1 + half) % 2, first=False, last=False)
            step(NG - 1, (NG - 1) % 2, first=False, last=True)

        @block.sync
        def _(sp):
            def at(groups, g):
                if isinstance(g, int):
                    return groups[g]
                view = groups[bass.ds(g, 1)]
                return view.rearrange("a p t d -> (a p) t d") if len(view.shape) == 4 else \
                    view.rearrange("a q p t d -> (a q) p t d")

            def load_quarters(g, par):
                quarters = at(x_quarters, g)
                for q in range(NQ):
                    sp.dma_start(x_quart[par][q * S:(q + 1) * S, :, :], quarters[q]).then_inc(quart_loaded[par], 16)

            sp.dma_start(cond_sb[:, :], cond).then_inc(cond_loaded, 16)
            sp.dma_start(W3_sb[:, :, :], W3.rearrange("(k p) d -> p k d", p=P)).then_inc(W3_loaded, 16)
            load_quarters(0, 0)
            for c in range(KC):
                sp.dma_start(W2_f[:, c, :], W2.rearrange("(p c) n -> p c n", c=KC)[:, c, :]).then_inc(W2_loaded[c], 16)
            sp.dma_start(b2_sb[:, :], b2.rearrange("(k p) -> p k", p=P), allow_slow_non_contiguous=True).then_inc(b2_loaded, 16)
            sp.wait_ge(zeroed, 4)
            sp.dma_start(Wd_f[:, :, 0:E], W_router.rearrange("(k p) e -> p k e", p=P)).then_inc(Wd_loaded, 16)
            sp.dma_start(Wd_f[:, :, SH:SH + R], A_s.rearrange("(k p) r -> p k r", p=P)).then_inc(Wd_loaded, 16)
            for k in range(KC):
                sp.dma_start(Wd_f[:, k, RO:P].rearrange("p (e r) -> p e r", r=R),
                             A_r[:, k * P:(k + 1) * P, :].rearrange("e p r -> p e r")).then_inc(Wd_loaded, 16)
            sp.dma_start(Wb_f[:, :, :], W_base.rearrange("(k p) d -> p k d", p=P)).then_inc(Wb_loaded, 16)
            load_quarters(1, 1)
            sp.dma_start(Wu_f[ONE:ONE + 1, :], b_base.rearrange("(a d) -> a d", a=1)).then_inc(Wu_loaded, 16)
            sp.dma_start(Wu_f[SH:SH + R, :], B_s).then_inc(Wu_loaded, 16)
            sp.dma_start(Wu_f[RO:P, :], B_r.rearrange("e r d -> (e r) d")).then_inc(Wu_loaded, 16)
            sp.dma_start(x_nat[0][:, :, :], x_groups[0]).then_inc(x_loaded[0], 16)

            def step(g, par):
                if not (isinstance(g, int) and g + 2 >= NG):
                    sp.wait_ge(xT_ready, KC * g + KC)
                    load_quarters(g + 2, par)
                if not (isinstance(g, int) and g + 1 >= NG):
                    if not (isinstance(g, int) and g == 0):
                        sp.wait_ge(out_ready, TT * g)
                    sp.dma_start(x_nat[1 - par][:, :, :], at(x_groups, g + 1)).then_inc(x_loaded[1 - par], 16)
                for t in range(TT):
                    sp.wait_ge(out_ready, TT * g + t + 1)
                    sp.dma_start(at(out_groups, g)[:, t, :], out_nat[par][:, t, :]).then_inc(stored[par], 16)

            step(0, 0)
            with sp.Fori(0, (NG - 4) // 2) as pair:
                for half in range(2):
                    step(pair * 2 + (1 + half), (1 + half) % 2)
            for g in range(NG - 3, NG):
                step(g, g % 2)
            for par in range(2):
                sp.wait_ge(stored[par], 16 * TT * (NG // 2))

        @block.gpsimd
        def _(pool):
            nc.gpsimd.memset(ident[:, :], 0.0).then_inc(zeroed, 1)
            nc.gpsimd.memset(earlier[:, :, :], 1.0).then_inc(zeroed, 1)
            nc.gpsimd.memset(Wd_f[:, :, :], 0.0).then_inc(zeroed, 1)
            nc.gpsimd.memset(Wu_f[:, :], 0.0).then_inc(zeroed, 1)
            pool.wait_ge(zeroed, 2)
            nc.gpsimd.affine_select(out=ident[:, :], in_=ident[:, :], compare_op=ALU.not_equal, fill=1.0,
                                    base=0, pattern=[[-1, P]], channel_multiplier=1).then_inc(ident_ready, 1)
            nc.gpsimd.affine_select(out=earlier[:, :, :], in_=earlier[:, :, :], compare_op=ALU.is_gt, fill=0.0,
                                    base=0, pattern=[[1, E], [-1, E]], channel_multiplier=0).then_inc(const_ready, 1)
            nc.gpsimd.memset(w_nat[:, :, 0:RO], 0.0).then_inc(zeroed, 1)
            pool.wait_ge(zeroed, 5)
            nc.gpsimd.memset(w_nat[:, :, ONE:ONE + 1], 1.0).then_inc(const_ready, 1)
            nc.gpsimd.memset(w_nat[:, :, SH:SH + R], 1.0).then_inc(const_ready, 1)

            def scale(g, c):
                n = KC * g + c
                pool.wait_ge(x1_sum_ready, n + 1)
                if not (isinstance(g, int) and g == 0):
                    pool.wait_ge(x1_lo_ready, n + 1 - KC)
                nc.gpsimd.tensor_tensor(per_batch(x1_full[:, c, :]), per_batch(x1_sum[:, c, :]),
                                        qT[:, c, bass.ds(BG * g, BG)].unsqueeze(2).to_broadcast([P, BG, N]),
                                        ALU.mult).then_inc(x1_full_ready, 1)

            def W_rest(lo, full, hi, n, ready):
                pool.wait_ge(W_hi_ready, n)
                nc.gpsimd.tensor_tensor(lo, full, hi.bitcast(F32), ALU.subtract).then_inc(ready, 1)

            pool.wait_ge(qT_ready, KC)
            for c in range(KC):
                scale(0, c)
                W_rest(W2_lo[:, c, :], W2_f[:, c, :], W2_hi[:, c, :], c + 1, W2_lo_ready)
            W_rest(Wd_lo[:, :, :], Wd_f[:, :, :], Wd_hi[:, :, :], KC + 1, Wd_lo_ready)
            scale(1, 0)
            scale(1, 1)
            W_rest(Wu_lo[:, :], Wu_f[:, :], Wu_hi[:, :], 2 * KC + 2, Wu_lo_ready)
            for c in range(2, KC):
                scale(1, c)
            with pool.Fori(2, NG) as g:
                for c in range(KC):
                    scale(g, c)

        @block.scalar
        def _(act):
            act.dma_start(b3_sb[:, :], b3.rearrange("(p c) -> p c", c=KC)).then_inc(b3_loaded, 16)
            act.wait_ge(ident_ready, 1)
            nc.scalar.activation(h_bias[:, :], ident[:, ONE:ONE + 1], ACT.Copy).then_inc(bias_ready, 1)
            act.wait_ge(bias_ready, 1)
            act.dma_start(h_bias[0:E, :], b_router.rearrange("(e a) -> e a", a=1)).then_inc(bias_loaded, 16)

            act.wait_ge(b3_loaded, 16)
            act.wait_ge(q_done, 1)
            for c in range(KC):
                nc.scalar.activation(qT[:, c, :], gate_ps[:, c * B:(c + 1) * B], ACT.Relu,
                                     bias=b3_sb[:, c:c + 1]).then_inc(qT_ready, 1)

            def x1_split(g, par, c):
                act.wait_ge(x1_full_ready, KC * g + c + 1)
                nc.scalar.activation(x1_hi[par][:, c, :], x1_full[:, c, :], ACT.Copy).then_inc(x1_hi_ready, 1)

            def relu(g, m, first):
                n = KC * g + m
                act.wait_ge(m1_done, n + 1)
                if not (first and m < 2):
                    act.wait_ge(y_lo_ready, n - 1)
                nc.scalar.activation(y_full[m % 2][:, :], prod[m][:, :], ACT.Relu,
                                     bias=b2_sb[:, m:m + 1]).then_inc(y_full_ready, 1)
                nc.scalar.activation(y_hi[:, m, :], prod[m][:, :], ACT.Relu,
                                     bias=b2_sb[:, m:m + 1]).then_inc(y_hi_ready, 1)

            for k in range(KC):
                act.wait_ge(W2_loaded[k], 16)
                nc.scalar.activation(W2_hi[:, k, :], W2_f[:, k, :], ACT.Copy).then_inc(W_hi_ready, 1)
                x1_split(0, 0, k)
            act.wait_ge(Wd_loaded, 16 * (2 + KC))
            nc.scalar.activation(Wd_hi[:, :, :], Wd_f[:, :, :], ACT.Copy).then_inc(W_hi_ready, 1)
            act.wait_ge(Wb_loaded, 16)
            for k in range(KC):
                nc.scalar.activation(Wb_hi[:, k, :], Wb_f[:, k, :], ACT.Copy).then_inc(W_hi_ready, 1)
            act.wait_ge(Wu_loaded, 48)
            nc.scalar.activation(Wu_hi[:, :], Wu_f[:, :], ACT.Copy).then_inc(W_hi_ready, 1)
            act.wait_ge(b2_loaded, 16)
            act.wait_ge(bias_loaded, 16)

            def step(g, par, first, last):
                def split(c):
                    if not last:
                        x1_split(g + 1, 1 - par, c)

                relu(g, 0, first)
                relu(g, 1, first)
                if not first:
                    split(0)
                relu(g, 2, first)
                relu(g, 3, first)
                if first:
                    split(0)
                split(1)
                act.wait_ge(h_done, g + 1)
                if not first:
                    act.wait_ge(logit_ready, g)
                for q in range(NQ):
                    nc.scalar.activation(h_head[q * S:(q + 1) * S, :], hT[0:S, q * P:(q + 1) * P], ACT.Identity,
                                         bias=h_bias[0:S, 0:1]).then_inc(h_head_ready, 1)
                if not first:
                    act.wait_ge(hw_ready, g)
                nc.scalar.activation(h_sb[:, :], hT[:, :], ACT.Identity, bias=h_bias[:, 0:1]).then_inc(h_ready, 1)
                split(2)
                act.wait_ge(logit_ready, g + 1)
                nc.scalar.activation(expo[:, :, :], logit[:, :, :], ACT.Exp).then_inc(expo_ready, 1)
                act.wait_ge(hw_ready, g + 1)
                nc.scalar.activation(hw_hi[:, :], hw_full[:, :], ACT.Copy).then_inc(hw_hi_ready, 1)
                split(3)

            steps(act, step)

        @block.vector
        def _(dve):
            dve.wait_ge(condT_done, 1)
            nc.vector.tensor_copy(condT[:, :, :], hT[:, 0:QC * B].rearrange("p (k b) -> p k b", b=B)).then_inc(condT_copied, 1)

            def x1_sums(g, par, c, first=False):
                n = KC * g + c
                if c == 0:
                    dve.wait_ge(quart_loaded[par], nth(g, par, 16 * NQ))
                nc.vector.transpose(xT[c % 2][:, :], x_quart[par][:, :, :].rearrange("p b (i c) -> p c b i", c=KC)[:, c]).then_inc(xT_ready, 1)
                dve.wait_ge(xT_ready, n + 1)
                nc.vector.tensor_reduce(vsum[c % 2][:, :], per_batch(xT[c % 2][:, :]), AX.X,
                                        ALU.add).then_inc(vsum_ready, 1)
                dve.wait_ge(vsum_ready, n + 1)
                if not first:
                    dve.wait_ge(x1_full_ready, n + 1 - KC)
                nc.vector.scalar_tensor_tensor(
                    out=per_batch(x1_sum[:, c, :]), in0=per_batch(xT[c % 2][:, :]), scalar=float(N),
                    in1=vsum[c % 2][:, :].unsqueeze(2).to_broadcast([P, BG, N]),
                    op0=ALU.mult, op1=ALU.add).then_inc(x1_sum_ready, 1)

            def x1_rest(g, par, c):
                dve.wait_ge(x1_hi_ready, KC * g + c + 1)
                nc.vector.tensor_tensor(x1_lo[par][:, c, :], x1_full[:, c, :],
                                        x1_hi[par][:, c, :].bitcast(F32), ALU.subtract).then_inc(x1_lo_ready, 1)

            def y_rest(g, m):
                dve.wait_ge(y_hi_ready, KC * g + m + 1)
                nc.vector.tensor_tensor(y_lo[:, m, :], y_full[m % 2][:, :],
                                        y_hi[:, m, :].bitcast(F32), ALU.subtract).then_inc(y_lo_ready, 1)

            for c in range(KC):
                x1_sums(0, 0, c, first=True)
                if c:
                    x1_rest(0, 0, c - 1)
            x1_rest(0, 0, KC - 1)
            for k in range(KC):
                dve.wait_ge(W_hi_ready, KC + 2 + k)
                nc.vector.tensor_tensor(Wb_lo[:, k, :], Wb_f[:, k, :], Wb_hi[:, k, :].bitcast(F32),
                                        ALU.subtract).then_inc(Wb_lo_ready, 1)
            dve.wait_ge(const_ready, 3)

            def rank_experts(g):
                done = GATE_STEPS * g
                dve.wait_ge(h_head_ready, NQ * (g + 1))
                nc.vector.transpose(h_nat[:, :, :], h_head[:, :].rearrange("p (b i) -> p b i", i=S)).then_inc(gate_step, 1)
                dve.wait_ge(gate_step, done + 1)
                nc.vector.tensor_reduce(lmax[:, :], gate_logits, AX.X, ALU.max).then_inc(gate_step, 1)
                dve.wait_ge(gate_step, done + 2)
                nc.vector.tensor_tensor(logit[:, :, :], gate_logits,
                                        lmax[:, :].unsqueeze(2).to_broadcast([P, TT, E]),
                                        ALU.subtract).then_inc(logit_ready, 1)
                dve.wait_ge(logit_ready, g + 1)
                nc.vector.tensor_tensor(diff[:, :, :, :],
                                        logit[:, :, :].unsqueeze(2).to_broadcast([P, TT, E, E]),
                                        logit[:, :, :].unsqueeze(3).to_broadcast([P, TT, E, E]),
                                        ALU.subtract).then_inc(gate_step, 1)
                dve.wait_ge(gate_step, done + 3)
                flat = "p t e j -> p t (e j)"
                nc.vector.scalar_tensor_tensor(
                    out=tie[:, :, :, :].rearrange(flat), in0=diff[:, :, :, :].rearrange(flat), scalar=0.0,
                    in1=earlier[:, :, :].rearrange("p e j -> p (e j)").unsqueeze(1).to_broadcast([P, TT, E * E]),
                    op0=ALU.is_ge, op1=ALU.mult).then_inc(gate_step, 1)
                dve.wait_ge(gate_step, done + 4)
                nc.vector.scalar_tensor_tensor(
                    out=beats[:, :, :, :].rearrange(flat), in0=diff[:, :, :, :].rearrange(flat), scalar=0.0,
                    in1=tie[:, :, :, :].rearrange(flat), op0=ALU.is_gt, op1=ALU.max).then_inc(gate_step, 1)
                dve.wait_ge(gate_step, done + 5)
                nc.vector.tensor_reduce(rank[:, :, :], beats[:, :, :, :], AX.X, ALU.add).then_inc(gate_step, 1)

            def gates(g, first):
                done = GATE_STEPS * g
                dve.wait_ge(expo_ready, g + 1)
                nc.vector.tensor_reduce(den[:, :], expo[:, :, :], AX.X, ALU.add).then_inc(gate_step, 1)
                dve.wait_ge(gate_step, done + 7)
                nc.vector.scalar_tensor_tensor(out=expo_top[:, :, :], in0=rank[:, :, :], scalar=1.5,
                                               in1=expo[:, :, :], op0=ALU.is_lt, op1=ALU.mult).then_inc(gate_step, 1)
                nc.vector.reciprocal(rden[:, :], den[:, :]).then_inc(gate_step, 1)
                dve.wait_ge(gate_step, done + 9)
                if not first:
                    dve.wait_ge(wT_done, g)
                nc.vector.tensor_tensor(w_nat[:, :, RO:P].rearrange("p t (e r) -> p t e r", r=R),
                                        expo_top[:, :, :].unsqueeze(3).to_broadcast([P, TT, E, R]),
                                        rden[:, :].unsqueeze(2).unsqueeze(3).to_broadcast([P, TT, E, R]),
                                        ALU.mult).then_inc(w_ready, 1)

            def step(g, par, first, last):
                def sums(c):
                    if not last:
                        x1_sums(g + 1, 1 - par, c)

                def rest(c):
                    if not last:
                        x1_rest(g + 1, 1 - par, c)

                if first:
                    sums(0)
                    sums(1)
                    for m in range(KC):
                        y_rest(g, m)
                    rest(0)
                else:
                    y_rest(g, 0)
                    sums(0)
                    y_rest(g, 1)
                    sums(1)
                    rest(0)
                    y_rest(g, 2)
                    y_rest(g, 3)
                sums(2)
                rank_experts(g)
                gates(g, first)
                sums(3)
                dve.wait_ge(wT_done, g + 1)
                if not first:
                    dve.wait_ge(hw_hi_ready, g)
                dve.wait_ge(h_ready, g + 1)
                nc.vector.tensor_tensor(hw_full[:, :], h_sb[:, :], gate_ps[:, :], ALU.mult).then_inc(hw_ready, 1)
                rest(1)
                dve.wait_ge(hw_hi_ready, g + 1)
                nc.vector.tensor_tensor(hw_lo[:, :], hw_full[:, :], hw_hi[:, :].bitcast(F32),
                                        ALU.subtract).then_inc(hw_lo_ready, 1)
                rest(2)
                rest(3)
                if not (isinstance(g, int) and g < 2):
                    dve.wait_ge(stored[par], (g - par) * (8 * TT))
                dve.wait_ge(x_loaded[par], nth(g, par, 16))
                for t in range(TT):
                    dve.wait_ge(m2_done, TT * g + t + 1)
                    nc.vector.tensor_tensor(out_nat[par][:, t, :], prod[t][:, :], x_nat[par][:, t, :],
                                            ALU.add).then_inc(out_ready, 1)

            step(0, 0, first=True, last=False)
            step(1, 1, first=False, last=False)
            with dve.Fori(0, (NG - 4) // 2) as pair:
                for half in range(2):
                    step(pair * 2 + (2 + half), half, first=False, last=False)
            step(NG - 2, 0, first=False, last=False)
            step(NG - 1, 1, first=False, last=True)

        @block.tensor
        def _(pe):
            pe.wait_ge(ident_ready, 1)
            pe.wait_ge(cond_loaded, 16)
            for k in range(QC):
                last = nc.tensor.transpose(hT[:, k * B:(k + 1) * B], cond_sb[:, k * P:(k + 1) * P], ident[0:B, 0:B])
            last.then_inc(condT_done, 1)

            def product(psum, terms, start, stop):
                for i, (lhsT, rhs) in enumerate(terms):
                    mm = nc.tensor.matmul(psum, lhsT, rhs, start=start and i == 0,
                                          stop=stop and i == len(terms) - 1)
                return mm

            def m1(g, par, m):
                cols = slice(m * P, (m + 1) * P)
                pe.wait_ge(out_ready, TT * (g - 1) + m + 1)
                for k in range(KC):
                    if m == 0:
                        pe.wait_ge(x1_lo_ready, KC * g + k + 1)
                    mm = product(prod[m][:, :], [(W2_hi[:, k, cols], x1_hi[par][:, k, :]),
                                                 (W2_hi[:, k, cols], x1_lo[par][:, k, :]),
                                                 (W2_lo[:, k, cols], x1_hi[par][:, k, :])], k == 0, k == KC - 1)
                mm.then_inc(m1_done, 1)

            def m1_first():
                def chunk(m, k):
                    cols = slice(m * P, (m + 1) * P)
                    return product(prod[m][:, :], [(W2_hi[:, k, cols], x1_hi[0][:, k, :]),
                                                   (W2_hi[:, k, cols], x1_lo[0][:, k, :]),
                                                   (W2_lo[:, k, cols], x1_hi[0][:, k, :])], k == 0, k == KC - 1)

                for k in range(KC // 2):
                    pe.wait_ge(W2_lo_ready, k + 1)
                    pe.wait_ge(x1_lo_ready, k + 1)
                    for m in range(KC):
                        chunk(m, k)
                for m in range(KC):
                    for k in range(KC // 2, KC):
                        if m == 0:
                            pe.wait_ge(W2_lo_ready, k + 1)
                            pe.wait_ge(x1_lo_ready, k + 1)
                        mm = chunk(m, k)
                    mm.then_inc(m1_done, 1)

            def h(g, k, first):
                if k == 0 and first:
                    pe.wait_ge(Wd_lo_ready, 1)
                elif k == 0:
                    pe.wait_ge(h_ready, g)
                pe.wait_ge(y_lo_ready, KC * g + k + 1)
                mm = product(hT[:, :], [(Wd_hi[:, k, :], y_hi[:, k, :]),
                                        (Wd_hi[:, k, :], y_lo[:, k, :]),
                                        (Wd_lo[:, k, :], y_hi[:, k, :])], k == 0, k == KC - 1)
                if k == KC - 1:
                    mm.then_inc(h_done, 1)

            def m2(t, k, first):
                toks = slice(t * P, (t + 1) * P)
                if first and t == 0:
                    pe.wait_ge(Wb_lo_ready, k + 1)
                product(prod[t][:, :], [(y_hi[:, k, toks], Wb_hi[:, k, :]),
                                        (y_hi[:, k, toks], Wb_lo[:, k, :]),
                                        (y_lo[:, k, toks], Wb_hi[:, k, :])], k == 0, False)

            def up(t):
                toks = slice(t * P, (t + 1) * P)
                product(prod[t][:, :], [(hw_hi[:, toks], Wu_hi[:, :]),
                                        (hw_hi[:, toks], Wu_lo[:, :]),
                                        (hw_lo[:, toks], Wu_hi[:, :])], False, True).then_inc(m2_done, 1)

            pe.wait_ge(W3_loaded, 16)
            pe.wait_ge(condT_copied, 1)
            for c in range(KC):
                for k in range(QC):
                    last = nc.tensor.matmul(gate_ps[:, c * B:(c + 1) * B],
                                            W3_sb[:, k, :].rearrange("p (f c) -> p c f", c=KC)[:, c],
                                            condT[:, k, :], start=(k == 0), stop=(k == QC - 1))
            last.then_inc(q_done, 1)

            def step(g, par, first, last):
                if first:
                    m1_first()
                else:
                    for m in range(KC):
                        m1(g, par, m)
                for k in range(KC - 1):
                    h(g, k, first)
                m2(0, 0, first)
                m2(0, 1, first)
                h(g, KC - 1, first)
                m2(0, 2, first)
                m2(0, 3, first)
                for k in range(KC):
                    m2(1, k, first)
                for k in range(KC // 2):
                    m2(2, k, first)
                pe.wait_ge(w_ready, g + 1)
                gate_cols = gate_ps[:, :].rearrange("r (q b i) -> r b q i", q=NQ, i=S)
                for b in range(TT):
                    mm = nc.tensor.transpose(gate_cols[:, b], w_nat[:, b, :], ident[:, :])
                mm.then_inc(wT_done, 1)
                for k in range(KC // 2, KC):
                    m2(2, k, first)
                for k in range(KC):
                    m2(3, k, first)
                if first:
                    pe.wait_ge(Wu_lo_ready, 1)
                pe.wait_ge(hw_lo_ready, g + 1)
                for t in range(TT):
                    up(t)

            steps(pe, step)


_INS = ['x', 'cond_1024', 'L0_cond_W3', 'L0_cond_b3', 'L0_cond_W2', 'L0_cond_b2', 'L0_ffn_W_base', 'L0_ffn_b_base',
        'L0_ffn_A_s', 'L0_ffn_B_s', 'L0_ffn_A_r', 'L0_ffn_B_r', 'L0_ffn_W_router', 'L0_ffn_b_router']
_OUTS = [((64, 64, 512), 'float32')]


def kernel(**inputs):
    import numpy as _np
    import concourse.bacc as _bacc
    from concourse import mybir as _mybir
    from concourse.bass_utils import run_bass_kernel_spmd as _run

    nc = _bacc.Bacc("TRN2", target_bir_lowering=False, num_devices=1)
    arrays, args = {}, []
    for name in _INS:
        a = _np.ascontiguousarray(inputs[name])
        arrays[f"in_{name}_dram"] = a
        args.append(nc.dram_tensor(f"in_{name}_dram", a.shape, _mybir.dt.from_np(a.dtype), kind="ExternalInput").ap())
    for i, (shape, dtype) in enumerate(_OUTS):
        dt = _mybir.dt.from_np(_np.dtype(dtype))
        args.append(nc.dram_tensor(f"out_{i}_dram", shape, dt, kind="ExternalOutput").ap())
    adaln_ffn(nc, *args)
    r = _run(nc, [arrays], core_ids=[0])
    return r.results[0]["out_0_dram"]
```

```python
import concourse.bass as bass
from concourse import mybir
from contextlib import ExitStack


def adaln_ffn(nc, x, cond, W3, b3, W2, b2, W_base, b_base, A_s, B_s, A_r, B_r, W_router, b_router, out):
    F32 = mybir.dt.float32
    F32R = mybir.dt.float32r
    ALU = mybir.AluOpType
    ACT = mybir.ActivationFunctionType
    AX = mybir.AxisListType

    P = 128
    B, N, D = x.shape
    Q = cond.shape[1]
    E, _, R = A_r.shape
    KC = D // P
    QC = Q // P
    TG = 512
    TT = TG // P
    BG = TG // N
    NG = B * N // TG
    S = 32
    NQ = P // S
    ONE = E
    SH = 16
    RO = 32
    WARM_LOAD, WARM_COPY, WARM_SPLIT = 12, 6, 3
    assert ONE < SH and SH + R <= RO and RO + E * R == P and TT == KC and NG % 2 == 0 and NG >= 4

    x_groups = x.rearrange("b n d -> (b n) d").rearrange("(g t p) d -> g p t d", t=TT, p=P)
    x_quarters = x.rearrange("b n d -> (b n) d").rearrange("(g b i) (q f) -> g q i b f", b=TG // S, i=S, q=NQ)
    out_groups = out.rearrange("b n d -> (b n) d").rearrange("(g t p) d -> g p t d", t=TT, p=P)

    ctx = ExitStack()
    with ctx:
        def sb(name, shape, dt=F32):
            return ctx.enter_context(nc.sbuf_tensor(name, shape, dt))

        def bank(name):
            return ctx.enter_context(nc.psum_tensor(name, [P, 512], F32))

        def sem(name):
            return ctx.enter_context(nc.semaphore(name))

        x_nat = [sb(f"x_nat{i}", [P, TT, D]) for i in range(2)]
        x_quart = [sb(f"x_quart{i}", [P, TG // S, KC * S]) for i in range(2)]
        xT = [sb(f"xT{i}", [P, TG]) for i in range(2)]
        out_nat = [sb(f"out_nat{i}", [P, TT, D]) for i in range(2)]
        vsum = [sb(f"vsum{i}", [P, BG]) for i in range(2)]
        x1_sum = sb("x1_sum", [P, KC, TG])
        x1_full = sb("x1_full", [P, KC, TG])
        x1_hi = [sb(f"x1_hi{i}", [P, KC, TG], F32R) for i in range(2)]
        x1_lo = [sb(f"x1_lo{i}", [P, KC, TG], F32R) for i in range(2)]
        y_full = [sb(f"y_full{i}", [P, TG]) for i in range(2)]
        y_hi = sb("y_hi", [P, KC, TG], F32R)
        y_lo = sb("y_lo", [P, KC, TG], F32R)
        h_sb = sb("h_sb", [P, TG])
        h_head = sb("h_head", [P, P])
        h_nat = sb("h_nat", [P, TT, S])
        gate_logits = h_nat[:, :, 0:E]
        hw_full = sb("hw_full", [P, TG])
        hw_hi = sb("hw_hi", [P, TG], F32R)
        hw_lo = sb("hw_lo", [P, TG], F32R)

        W2_f = sb("W2_f", [P, KC, D])
        Wb_f = sb("Wb_f", [P, KC, D])
        Wd_f = sb("Wd_f", [P, KC, P])
        Wu_f = sb("Wu_f", [P, D])
        W2_hi = sb("W2_hi", [P, KC, D], F32R)
        W2_lo = sb("W2_lo", [P, KC, D], F32R)
        Wb_hi = sb("Wb_hi", [P, KC, D], F32R)
        Wb_lo = sb("Wb_lo", [P, KC, D], F32R)
        Wd_hi = sb("Wd_hi", [P, KC, P], F32R)
        Wd_lo = sb("Wd_lo", [P, KC, P], F32R)
        Wu_hi = sb("Wu_hi", [P, D], F32R)
        Wu_lo = sb("Wu_lo", [P, D], F32R)
        idle = sb("idle", [P, 512], mybir.dt.bfloat16)
        W3_sb = sb("W3_sb", [P, QC, D])
        cond_sb = sb("cond_sb", [B, Q])
        condT = sb("condT", [P, QC, B])
        qT = sb("qT", [P, KC, B])
        b3_sb = sb("b3_sb", [P, KC])
        b2_sb = sb("b2_sb", [P, KC])
        h_bias = sb("h_bias", [P, 1])
        ident = sb("ident", [P, P])
        earlier = sb("earlier", [P, E, E])

        lmax = sb("lmax", [P, TT])
        logit = sb("logit", [P, TT, E])
        diff = sb("diff", [P, TT, E, E])
        tie = sb("tie", [P, TT, E, E])
        beats = sb("beats", [P, TT, E, E])
        rank = sb("rank", [P, TT, E])
        expo = sb("expo", [P, TT, E])
        expo_top = sb("expo_top", [P, TT, E])
        den = sb("den", [P, TT])
        rden = sb("rden", [P, TT])
        w_nat = sb("w_nat", [P, TT, E * R])
        gatesT = sb("gatesT", [P, TG])

        m2_ps = [bank(f"m2_ps{t}") for t in range(TT)]
        m1_ps = [bank(f"m1_ps{m}") for m in range(KC - 1)] + [m2_ps[2]]
        hT = bank("hT")
        q_ps = [hT, m2_ps[0], m2_ps[1], m2_ps[3]]

        x_loaded = [sem(f"x_loaded{i}") for i in range(2)]
        quart_loaded = [sem(f"quart_loaded{i}") for i in range(2)]
        stored = [sem(f"stored{i}") for i in range(2)]
        cond_loaded, W3_loaded, b3_loaded, b2_loaded = sem("cond_loaded"), sem("W3_loaded"), sem("b3_loaded"), sem("b2_loaded")
        W2_loaded = [sem(f"W2_loaded{c}") for c in range(KC)]
        Wb_loaded, Wd_loaded, Wu_loaded = sem("Wb_loaded"), sem("Wd_loaded"), sem("Wu_loaded")
        bias_loaded = sem("bias_loaded")
        idle_ready = sem("idle_ready")
        zeroed, ident_ready, const_ready = sem("zeroed"), sem("ident_ready"), sem("const_ready")
        bias_ready = sem("bias_ready")
        condT_done, condT_copied, q_done, qT_ready = sem("condT_done"), sem("condT_copied"), sem("q_done"), sem("qT_ready")
        W_hi_ready = sem("W_hi_ready")
        W2_lo_ready, Wb_lo_ready, Wd_lo_ready, Wu_lo_ready = sem("W2_lo_ready"), sem("Wb_lo_ready"), sem("Wd_lo_ready"), sem("Wu_lo_ready")
        xT_ready, vsum_ready, x1_sum_ready, x1_full_ready = sem("xT_ready"), sem("vsum_ready"), sem("x1_sum_ready"), sem("x1_full_ready")
        x1_hi_ready, x1_lo_ready = sem("x1_hi_ready"), sem("x1_lo_ready")
        m1_done, y_full_ready, y_hi_ready, y_lo_ready = sem("m1_done"), sem("y_full_ready"), sem("y_hi_ready"), sem("y_lo_ready")
        h_done, h_ready = sem("h_done"), sem("h_ready")
        h_head_ready, logit_ready, expo_ready, gate_step = sem("h_head_ready"), sem("logit_ready"), sem("expo_ready"), sem("gate_step")
        w_ready, wT_done = sem("w_ready"), sem("wT_done")
        hw_ready, hw_hi_ready, hw_lo_ready = sem("hw_ready"), sem("hw_hi_ready"), sem("hw_lo_ready")
        m2_done, out_ready = sem("m2_done"), sem("out_ready")

        GATE_STEPS = 9

        block = ctx.enter_context(nc.Block())

        def per_batch(ap):
            return ap.rearrange("p (b n) -> p b n", n=N)


        def nth(g, par, unit):
            return (g - par) * (unit // 2) + unit

        def steps(eng, step):
            for g in range(3):
                step(g, g % 2)
            with eng.Fori(0, (NG - 4) // 2) as pair:
                for half in range(2):
                    step(pair * 2 + (3 + half), (3 + half) % 2)
            step(NG - 1, (NG - 1) % 2)

        def place(g):
            return tuple(isinstance(g, int) and g == n for n in (0, 1, NG - 1))

        @block.sync
        def _(sp):
            def at(groups, g):
                if isinstance(g, int):
                    return groups[g]
                view = groups[bass.ds(g, 1)]
                return view.rearrange("a p t d -> (a p) t d") if len(view.shape) == 4 else \
                    view.rearrange("a q p t d -> (a q) p t d")

            def load_quarters(g, par):
                quarters = at(x_quarters, g)
                for q in range(NQ):
                    sp.dma_start(x_quart[par][q * S:(q + 1) * S, :, :], quarters[q]).then_inc(quart_loaded[par], 16)

            load_quarters(0, 0)
            sp.dma_start(cond_sb[:, :], cond).then_inc(cond_loaded, 16)
            sp.dma_start(W3_sb[:, :, :], W3.rearrange("(k p) d -> p k d", p=P)).then_inc(W3_loaded, 16)
            for c in range(KC):
                sp.dma_start(W2_f[:, c, :], W2.rearrange("(p c) n -> p c n", c=KC)[:, c, :]).then_inc(W2_loaded[c], 16)
            sp.dma_start(b2_sb[:, :], b2.rearrange("(k p) -> p k", p=P), allow_slow_non_contiguous=True).then_inc(b2_loaded, 16)
            sp.wait_ge(zeroed, 4)
            sp.dma_start(Wd_f[:, :, 0:E], W_router.rearrange("(k p) e -> p k e", p=P)).then_inc(Wd_loaded, 16)
            sp.dma_start(Wd_f[:, :, SH:SH + R], A_s.rearrange("(k p) r -> p k r", p=P)).then_inc(Wd_loaded, 16)
            for k in range(KC):
                sp.dma_start(Wd_f[:, k, RO:P].rearrange("p (e r) -> p e r", r=R),
                             A_r[:, k * P:(k + 1) * P, :].rearrange("e p r -> p e r")).then_inc(Wd_loaded, 16)
            sp.dma_start(Wb_f[:, :, :], W_base.rearrange("(k p) d -> p k d", p=P)).then_inc(Wb_loaded, 16)
            load_quarters(1, 1)
            sp.dma_start(Wu_f[ONE:ONE + 1, :], b_base.rearrange("(a d) -> a d", a=1)).then_inc(Wu_loaded, 16)
            sp.dma_start(Wu_f[SH:SH + R, :], B_s).then_inc(Wu_loaded, 16)
            sp.dma_start(Wu_f[RO:P, :], B_r.rearrange("e r d -> (e r) d")).then_inc(Wu_loaded, 16)
            sp.dma_start(x_nat[0][:, :, :], x_groups[0]).then_inc(x_loaded[0], 16)

            def store(g, par):
                for t in range(TT):
                    sp.wait_ge(out_ready, TT * g + t + 1)
                    sp.dma_start(at(out_groups, g)[:, t, :], out_nat[par][:, t, :]).then_inc(stored[par], 16)

            def step(g, par, first=False):
                if not (isinstance(g, int) and g + 2 >= NG):
                    sp.wait_ge(xT_ready, KC * g + KC)
                    load_quarters(g + 2, par)
                if not first:
                    store(g - 1, 1 - par)
                if not (isinstance(g, int) and g + 1 >= NG):
                    sp.dma_start(x_nat[1 - par][:, :, :], at(x_groups, g + 1)).then_inc(x_loaded[1 - par], 16)

            step(0, 0, first=True)
            with sp.Fori(0, (NG - 4) // 2) as pair:
                for half in range(2):
                    step(pair * 2 + (1 + half), (1 + half) % 2)
            for g in range(NG - 3, NG):
                step(g, g % 2)
            store(NG - 1, (NG - 1) % 2)
            for par in range(2):
                sp.wait_ge(stored[par], 16 * TT * (NG // 2))

        @block.gpsimd
        def _(pool):
            nc.gpsimd.memset(ident[:, :], 0.0).then_inc(zeroed, 1)
            nc.gpsimd.memset(earlier[:, :, :], 1.0).then_inc(zeroed, 1)
            nc.gpsimd.memset(Wd_f[:, :, :], 0.0).then_inc(zeroed, 1)
            nc.gpsimd.memset(Wu_f[:, :], 0.0).then_inc(zeroed, 1)
            pool.wait_ge(zeroed, 2)
            nc.gpsimd.affine_select(out=ident[:, :], in_=ident[:, :], compare_op=ALU.not_equal, fill=1.0,
                                    base=0, pattern=[[-1, P]], channel_multiplier=1).then_inc(ident_ready, 1)
            nc.gpsimd.affine_select(out=earlier[:, :, :], in_=earlier[:, :, :], compare_op=ALU.is_gt, fill=0.0,
                                    base=0, pattern=[[1, E], [-1, E]], channel_multiplier=0).then_inc(const_ready, 1)
            nc.gpsimd.memset(gatesT[0:RO, :], 1.0).then_inc(const_ready, 1)

            def scale(g, c):
                n = KC * g + c
                pool.wait_ge(x1_sum_ready, n + 1)
                if not (isinstance(g, int) and g == 0):
                    pool.wait_ge(x1_lo_ready, n + 1 - KC)
                nc.gpsimd.tensor_tensor(per_batch(x1_full[:, c, :]), per_batch(x1_sum[:, c, :]),
                                        qT[:, c, bass.ds(BG * g, BG)].unsqueeze(2).to_broadcast([P, BG, N]),
                                        ALU.mult).then_inc(x1_full_ready, 1)

            def W_rest(lo, full, hi, n, ready):
                pool.wait_ge(W_hi_ready, n)
                nc.gpsimd.tensor_tensor(lo, full, hi.bitcast(F32), ALU.subtract).then_inc(ready, 1)

            for c in range(KC):
                if c:
                    pool.wait_ge(qT_ready, c + 1)
                    scale(0, c)
                W_rest(W2_lo[:, c, :], W2_f[:, c, :], W2_hi[:, c, :], c + 1, W2_lo_ready)
            W_rest(Wd_lo[:, :, :], Wd_f[:, :, :], Wd_hi[:, :, :], KC + 1, Wd_lo_ready)
            for k in range(KC):
                W_rest(Wb_lo[:, k, :], Wb_f[:, k, :], Wb_hi[:, k, :], KC + 2 + k, Wb_lo_ready)
            scale(1, 0)
            scale(1, 1)
            W_rest(Wu_lo[:, :], Wu_f[:, :], Wu_hi[:, :], 2 * KC + 2, Wu_lo_ready)
            for c in range(2, KC):
                scale(1, c)
            with pool.Fori(2, NG) as g:
                for c in range(KC):
                    scale(g, c)

        @block.scalar
        def _(act):
            act.dma_start(b3_sb[:, :], b3.rearrange("(p c) -> p c", c=KC)).then_inc(b3_loaded, 16)
            act.wait_ge(ident_ready, 1)
            nc.scalar.activation(h_bias[:, :], ident[:, ONE:ONE + 1], ACT.Copy).then_inc(bias_ready, 1)
            act.wait_ge(bias_ready, 1)
            act.dma_start(h_bias[0:E, :], b_router.rearrange("(e a) -> e a", a=1)).then_inc(bias_loaded, 16)

            def x1_split(g, par, c):
                act.wait_ge(x1_full_ready, KC * g + c + 1)
                nc.scalar.activation(x1_hi[par][:, c, :], x1_full[:, c, :], ACT.Copy).then_inc(x1_hi_ready, 1)

            def relu(g, m, first):
                n = KC * g + m
                act.wait_ge(m1_done, n + 1)
                if not (first and m < 2):
                    act.wait_ge(y_lo_ready, n - 1)
                nc.scalar.activation(y_full[m % 2][:, :], m1_ps[m][:, :], ACT.Relu,
                                     bias=b2_sb[:, m:m + 1]).then_inc(y_full_ready, 1)
                nc.scalar.activation(y_hi[:, m, :], m1_ps[m][:, :], ACT.Relu,
                                     bias=b2_sb[:, m:m + 1]).then_inc(y_hi_ready, 1)

            act.wait_ge(condT_done, 1)
            nc.scalar.activation(condT[:, :, :], hT[:, 0:QC * B].rearrange("p (k b) -> p k b", b=B), ACT.Copy).then_inc(condT_copied, 1)
            act.wait_ge(b3_loaded, 16)
            for c in range(KC):
                act.wait_ge(q_done, c + 1)
                nc.scalar.activation(qT[:, c, :], q_ps[c][:, 0:B], ACT.Relu,
                                     bias=b3_sb[:, c:c + 1]).then_inc(qT_ready, 1)
                if c:
                    x1_split(0, 0, c - 1)
                act.wait_ge(W2_loaded[c], 16)
                nc.scalar.activation(W2_hi[:, c, :], W2_f[:, c, :], ACT.Copy).then_inc(W_hi_ready, 1)
            act.wait_ge(Wd_loaded, 16 * (2 + KC))
            nc.scalar.activation(Wd_hi[:, :, :], Wd_f[:, :, :], ACT.Copy).then_inc(W_hi_ready, 1)
            act.wait_ge(Wb_loaded, 16)
            for k in range(KC):
                if k == KC // 2:
                    x1_split(0, 0, KC - 1)
                nc.scalar.activation(Wb_hi[:, k, :], Wb_f[:, k, :], ACT.Copy).then_inc(W_hi_ready, 1)
            act.wait_ge(b2_loaded, 16)
            act.wait_ge(bias_loaded, 16)

            def step(g, par):
                first, second, last = place(g)

                def split(c):
                    if not last:
                        x1_split(g + 1, 1 - par, c)

                for m in range(KC):
                    relu(g, m, first)
                    if not first and m >= (2 if second else 1):
                        split(m - (2 if second else 1))
                if first:
                    act.wait_ge(Wu_loaded, 48)
                    nc.scalar.activation(Wu_hi[:, :], Wu_f[:, :], ACT.Copy).then_inc(W_hi_ready, 1)
                act.wait_ge(h_done, g + 1)
                if not first:
                    act.wait_ge(logit_ready, g)
                for q in range(NQ):
                    nc.scalar.activation(h_head[q * S:(q + 1) * S, :], hT[0:S, q * P:(q + 1) * P], ACT.Identity,
                                         bias=h_bias[0:S, 0:1]).then_inc(h_head_ready, 1)
                if not first:
                    act.wait_ge(hw_ready, g)
                nc.scalar.activation(h_sb[:, :], hT[:, :], ACT.Identity, bias=h_bias[:, 0:1]).then_inc(h_ready, 1)
                if first:
                    split(0)
                    split(1)
                if second:
                    split(2)
                act.wait_ge(logit_ready, g + 1)
                nc.scalar.activation(expo[:, :, :], logit[:, :, :], ACT.Exp).then_inc(expo_ready, 1)
                if first:
                    split(2)
                split(3)
                parts = 2 if last else 1
                for i in range(parts):
                    toks = slice(i * TG // parts, (i + 1) * TG // parts)
                    act.wait_ge(hw_ready, g + 1 + i)
                    nc.scalar.activation(hw_hi[:, toks], hw_full[:, toks], ACT.Copy).then_inc(hw_hi_ready, 1)

            steps(act, step)

        @block.vector
        def _(dve):
            nc.vector.memset(idle[:, :], 0.0).then_inc(idle_ready, 1)

            def turn_x(g, par, c):
                if c == 0:
                    dve.wait_ge(quart_loaded[par], nth(g, par, 16 * NQ))
                nc.vector.transpose(xT[c % 2][:, :], x_quart[par][:, :, :].rearrange("p b (i c) -> p c b i", c=KC)[:, c]).then_inc(xT_ready, 1)

            def sum_x(g, c):
                dve.wait_ge(xT_ready, KC * g + c + 1)
                nc.vector.tensor_reduce(vsum[c % 2][:, :], per_batch(xT[c % 2][:, :]), AX.X,
                                        ALU.add).then_inc(vsum_ready, 1)

            def add_sum(g, c):
                n = KC * g + c
                dve.wait_ge(vsum_ready, n + 1)
                if not (isinstance(g, int) and g == 0):
                    dve.wait_ge(x1_full_ready, n + 1 - KC)
                nc.vector.scalar_tensor_tensor(
                    out=per_batch(x1_sum[:, c, :]), in0=per_batch(xT[c % 2][:, :]), scalar=float(N),
                    in1=vsum[c % 2][:, :].unsqueeze(2).to_broadcast([P, BG, N]),
                    op0=ALU.mult, op1=ALU.add).then_inc(x1_sum_ready, 1)

            def x1_rest(g, par, c):
                dve.wait_ge(x1_hi_ready, KC * g + c + 1)
                nc.vector.tensor_tensor(x1_lo[par][:, c, :], x1_full[:, c, :],
                                        x1_hi[par][:, c, :].bitcast(F32), ALU.subtract).then_inc(x1_lo_ready, 1)

            def y_rest(g, m):
                dve.wait_ge(y_hi_ready, KC * g + m + 1)
                nc.vector.tensor_tensor(y_lo[:, m, :], y_full[m % 2][:, :],
                                        y_hi[:, m, :].bitcast(F32), ALU.subtract).then_inc(y_lo_ready, 1)

            turn_x(0, 0, 0)
            sum_x(0, 0)
            add_sum(0, 0)
            turn_x(0, 0, 1)
            sum_x(0, 1)
            dve.wait_ge(x1_sum_ready, 1)
            dve.wait_ge(qT_ready, 1)
            nc.vector.tensor_tensor(per_batch(x1_full[:, 0, :]), per_batch(x1_sum[:, 0, :]),
                                    qT[:, 0, 0:BG].unsqueeze(2).to_broadcast([P, BG, N]),
                                    ALU.mult).then_inc(x1_full_ready, 1)
            add_sum(0, 1)
            x1_rest(0, 0, 0)
            for c in range(2, KC):
                turn_x(0, 0, c)
                sum_x(0, c)
                add_sum(0, c)
                x1_rest(0, 0, c - 1)
            x1_rest(0, 0, KC - 1)
            dve.wait_ge(const_ready, 2)

            def rank_experts(g):
                done = GATE_STEPS * g
                dve.wait_ge(h_head_ready, NQ * (g + 1))
                nc.vector.transpose(h_nat[:, :, :], h_head[:, :].rearrange("p (b i) -> p b i", i=S)).then_inc(gate_step, 1)
                dve.wait_ge(gate_step, done + 1)
                nc.vector.tensor_reduce(lmax[:, :], gate_logits, AX.X, ALU.max).then_inc(gate_step, 1)
                dve.wait_ge(gate_step, done + 2)
                nc.vector.tensor_tensor(logit[:, :, :], gate_logits,
                                        lmax[:, :].unsqueeze(2).to_broadcast([P, TT, E]),
                                        ALU.subtract).then_inc(logit_ready, 1)
                dve.wait_ge(logit_ready, g + 1)
                nc.vector.tensor_tensor(diff[:, :, :, :],
                                        logit[:, :, :].unsqueeze(2).to_broadcast([P, TT, E, E]),
                                        logit[:, :, :].unsqueeze(3).to_broadcast([P, TT, E, E]),
                                        ALU.subtract).then_inc(gate_step, 1)
                dve.wait_ge(gate_step, done + 3)
                flat = "p t e j -> p t (e j)"
                nc.vector.scalar_tensor_tensor(
                    out=tie[:, :, :, :].rearrange(flat), in0=diff[:, :, :, :].rearrange(flat), scalar=0.0,
                    in1=earlier[:, :, :].rearrange("p e j -> p (e j)").unsqueeze(1).to_broadcast([P, TT, E * E]),
                    op0=ALU.is_ge, op1=ALU.mult).then_inc(gate_step, 1)
                dve.wait_ge(gate_step, done + 4)
                nc.vector.scalar_tensor_tensor(
                    out=beats[:, :, :, :].rearrange(flat), in0=diff[:, :, :, :].rearrange(flat), scalar=0.0,
                    in1=tie[:, :, :, :].rearrange(flat), op0=ALU.is_gt, op1=ALU.max).then_inc(gate_step, 1)
                dve.wait_ge(gate_step, done + 5)
                nc.vector.tensor_reduce(rank[:, :, :], beats[:, :, :, :], AX.X, ALU.add).then_inc(gate_step, 1)

            def gates(g):
                done = GATE_STEPS * g
                dve.wait_ge(expo_ready, g + 1)
                nc.vector.tensor_reduce(den[:, :], expo[:, :, :], AX.X, ALU.add).then_inc(gate_step, 1)
                dve.wait_ge(gate_step, done + 7)
                nc.vector.scalar_tensor_tensor(out=expo_top[:, :, :], in0=rank[:, :, :], scalar=1.5,
                                               in1=expo[:, :, :], op0=ALU.is_lt, op1=ALU.mult).then_inc(gate_step, 1)
                nc.vector.reciprocal(rden[:, :], den[:, :]).then_inc(gate_step, 1)
                dve.wait_ge(gate_step, done + 9)
                nc.vector.tensor_tensor(w_nat[:, :, :].rearrange("p t (e r) -> p t e r", r=R),
                                        expo_top[:, :, :].unsqueeze(3).to_broadcast([P, TT, E, R]),
                                        rden[:, :].unsqueeze(2).unsqueeze(3).to_broadcast([P, TT, E, R]),
                                        ALU.mult).then_inc(w_ready, 1)

            def turn_gates(g, quarters):
                for q in quarters:
                    for f in range(1, NQ):
                        nc.vector.transpose(gatesT[f * S:(f + 1) * S, q * P:(q + 1) * P],
                                            w_nat[q * S:(q + 1) * S, :, (f - 1) * S:f * S]).then_inc(wT_done, 1)
                dve.wait_ge(wT_done, (NQ - 1) * (NQ * g + q + 1))

            def weigh(g, toks, n):
                if not (isinstance(n, int) and n == 1):
                    dve.wait_ge(hw_hi_ready, n - 1)
                dve.wait_ge(h_ready, g + 1)
                nc.vector.tensor_tensor(hw_full[:, toks], h_sb[:, toks], gatesT[:, toks], ALU.mult).then_inc(hw_ready, 1)

            def hw_rest(toks, n):
                dve.wait_ge(hw_hi_ready, n)
                nc.vector.tensor_tensor(hw_lo[:, toks], hw_full[:, toks], hw_hi[:, toks].bitcast(F32),
                                        ALU.subtract).then_inc(hw_lo_ready, 1)

            def add_x(g, par, tiles):
                for t in tiles:
                    if t == 0:
                        if not (isinstance(g, int) and g < 2):
                            dve.wait_ge(stored[par], (g - par) * (8 * TT))
                        dve.wait_ge(x_loaded[par], nth(g, par, 16))
                    dve.wait_ge(m2_done, TT * g + t + 1)
                    nc.vector.tensor_tensor(out_nat[par][:, t, :], m2_ps[t][:, :], x_nat[par][:, t, :],
                                            ALU.add).then_inc(out_ready, 1)

            def step(g, par):
                first, second, last = place(g)

                def turn(*chunks):
                    for c in () if last else chunks:
                        turn_x(g + 1, 1 - par, c)

                def total(*chunks):
                    for c in () if last else chunks:
                        sum_x(g + 1, c)
                        add_sum(g + 1, c)

                def rest(*chunks):
                    for c in () if last else chunks:
                        x1_rest(g + 1, 1 - par, c)

                if first:
                    turn(0)
                    total(0)
                    y_rest(g, 0)
                    turn(1)
                    y_rest(g, 1)
                    sum_x(g + 1, 1)
                    y_rest(g, 2)
                    add_sum(g + 1, 1)
                    y_rest(g, 3)
                    turn(2)
                    total(2)
                elif second:
                    y_rest(g, 0)
                    add_x(g - 1, 1 - par, [0])
                    y_rest(g, 1)
                    add_x(g - 1, 1 - par, [1, 2, 3])
                    turn(0)
                    total(0)
                    turn(1)
                    y_rest(g, 2)
                    total(1)
                    rest(0)
                    y_rest(g, 3)
                    rest(1)
                    turn(2)
                    total(2)
                else:
                    turn(0)
                    total(0)
                    y_rest(g, 0)
                    turn(1)
                    add_x(g - 1, 1 - par, [0])
                    y_rest(g, 1)
                    add_x(g - 1, 1 - par, [1, 2, 3])
                    total(1)
                    rest(0)
                    turn(2)
                    y_rest(g, 2)
                    total(2)
                    rest(1)
                    turn(3)
                    y_rest(g, 3)
                    total(3)
                rank_experts(g)
                gates(g)
                if first:
                    rest(0)
                if first or second:
                    turn(3)
                    total(3)
                if first:
                    rest(1)
                dve.wait_ge(w_ready, g + 1)
                rest(2)
                if first or second:
                    turn_gates(g, [0, 1])
                    rest(3)
                    turn_gates(g, [2, 3])
                    weigh(g, slice(0, TG), g + 1)
                    hw_rest(slice(0, TG), g + 1)
                elif not last:
                    rest(3)
                    turn_gates(g, range(NQ))
                    weigh(g, slice(0, TG), g + 1)
                    hw_rest(slice(0, TG), g + 1)
                else:
                    front, back = slice(0, TG // 2), slice(TG // 2, TG)
                    turn_gates(g, [0, 1])
                    weigh(g, front, g + 1)
                    turn_gates(g, [2])
                    hw_rest(front, g + 1)
                    turn_gates(g, [3])
                    weigh(g, back, g + 2)
                    hw_rest(back, g + 2)

            steps(dve, step)
            add_x(NG - 1, (NG - 1) % 2, range(TT))

        @block.tensor
        def _(pe):
            def keep_warm(n):
                for _ in range(n):
                    nc.tensor.matmul(m2_ps[2][:, :], idle[:, 0:P], idle[:, :], start=True, stop=True)

            pe.wait_ge(idle_ready, 1)
            keep_warm(WARM_LOAD)
            pe.wait_ge(ident_ready, 1)
            pe.wait_ge(cond_loaded, 16)
            for k in range(QC):
                last = nc.tensor.transpose(hT[:, k * B:(k + 1) * B], cond_sb[:, k * P:(k + 1) * P], ident[0:B, 0:B])
            last.then_inc(condT_done, 1)
            keep_warm(WARM_COPY)

            def product(psum, terms, start, stop):
                for i, (lhsT, rhs) in enumerate(terms):
                    mm = nc.tensor.matmul(psum, lhsT, rhs, start=start and i == 0,
                                          stop=stop and i == len(terms) - 1)
                return mm

            def m1(g, par, m):
                cols = slice(m * P, (m + 1) * P)
                if m == KC - 1:
                    pe.wait_ge(out_ready, TT * (g - 1) + 3)
                for k in range(KC):
                    if m == 0:
                        pe.wait_ge(x1_lo_ready, KC * g + k + 1)
                    mm = product(m1_ps[m][:, :], [(W2_hi[:, k, cols], x1_hi[par][:, k, :]),
                                                 (W2_hi[:, k, cols], x1_lo[par][:, k, :]),
                                                 (W2_lo[:, k, cols], x1_hi[par][:, k, :])], k == 0, k == KC - 1)
                mm.then_inc(m1_done, 1)

            def m1_first():
                def chunk(m, k, W, x1):
                    return nc.tensor.matmul(m1_ps[m][:, :], W[:, k, m * P:(m + 1) * P], x1[0][:, k, :],
                                            start=k == 0 and W is W2_hi and x1 is x1_hi,
                                            stop=k == KC - 1 and x1 is x1_lo)

                for k in range(KC - 1):
                    pe.wait_ge(x1_hi_ready, k + 1)
                    pe.wait_ge(W_hi_ready, k + 1)
                    for m in range(KC):
                        chunk(m, k, W2_hi, x1_hi)
                    pe.wait_ge(W2_lo_ready, k + 1)
                    for m in range(KC):
                        chunk(m, k, W2_lo, x1_hi)
                    pe.wait_ge(x1_lo_ready, k + 1)
                    for m in range(KC):
                        chunk(m, k, W2_hi, x1_lo)
                pe.wait_ge(W2_lo_ready, KC)
                pe.wait_ge(x1_hi_ready, KC)
                for m in range(KC):
                    chunk(m, KC - 1, W2_hi, x1_hi)
                    chunk(m, KC - 1, W2_lo, x1_hi)
                    if m == 0:
                        pe.wait_ge(x1_lo_ready, KC)
                    chunk(m, KC - 1, W2_hi, x1_lo).then_inc(m1_done, 1)

            def h(g, k, first):
                if k == 0 and first:
                    pe.wait_ge(Wd_lo_ready, 1)
                elif k == 0:
                    pe.wait_ge(h_ready, g)
                pe.wait_ge(y_hi_ready, KC * g + k + 1)
                product(hT[:, :], [(Wd_hi[:, k, :], y_hi[:, k, :]),
                                   (Wd_lo[:, k, :], y_hi[:, k, :])], k == 0, False)
                pe.wait_ge(y_lo_ready, KC * g + k + 1)
                mm = product(hT[:, :], [(Wd_hi[:, k, :], y_lo[:, k, :])], False, k == KC - 1)
                if k == KC - 1:
                    mm.then_inc(h_done, 1)

            def m2(t, k, first):
                toks = slice(t * P, (t + 1) * P)
                if first and t == 0:
                    pe.wait_ge(Wb_lo_ready, k + 1)
                product(m2_ps[t][:, :], [(y_hi[:, k, toks], Wb_hi[:, k, :]),
                                        (y_hi[:, k, toks], Wb_lo[:, k, :]),
                                        (y_lo[:, k, toks], Wb_hi[:, k, :])], k == 0, False)

            def up(tiles, n):
                for i, t in enumerate(tiles):
                    toks = slice(t * P, (t + 1) * P)
                    if i == 0:
                        pe.wait_ge(hw_hi_ready, n)
                    product(m2_ps[t][:, :], [(hw_hi[:, toks], Wu_hi[:, :]),
                                            (hw_hi[:, toks], Wu_lo[:, :])], False, False)
                    if i == 0:
                        pe.wait_ge(hw_lo_ready, n)
                    product(m2_ps[t][:, :], [(hw_lo[:, toks], Wu_hi[:, :])], False, True).then_inc(m2_done, 1)

            pe.wait_ge(W3_loaded, 16)
            pe.wait_ge(condT_copied, 1)
            for c in range(KC):
                for k in range(QC):
                    mm = nc.tensor.matmul(q_ps[c][:, 0:B], W3_sb[:, k, :].rearrange("p (f c) -> p c f", c=KC)[:, c],
                                          condT[:, k, :], start=(k == 0), stop=(k == QC - 1))
                mm.then_inc(q_done, 1)
            keep_warm(WARM_SPLIT)

            def step(g, par):
                first, second, last = place(g)
                if first:
                    m1_first()
                else:
                    m1(g, par, 0)
                    m1(g, par, 1)
                    up(range(TT), g)
                    for m in range(2, KC):
                        m1(g, par, m)
                for k in range(KC - 1):
                    h(g, k, first)
                    if first:
                        m2(0, k, first)
                if not first:
                    m2(0, 0, first)
                    m2(0, 1, first)
                h(g, KC - 1, first)
                if not first:
                    m2(0, 2, first)
                m2(0, 3, first)
                if not first:
                    pe.wait_ge(out_ready, TT * g)
                others = [(t, k) for t in range(1, TT) for k in range(KC)]
                if not last:
                    for t, k in others:
                        m2(t, k, first)
                    if first:
                        pe.wait_ge(Wu_lo_ready, 1)
                else:
                    for t, k in others[:-3]:
                        m2(t, k, first)
                    up(range(TT // 2), g + 1)
                    for t, k in others[-3:]:
                        m2(t, k, first)
                    up(range(TT // 2, TT), g + 2)

            steps(pe, step)


_INS = ['x', 'cond_1024', 'L0_cond_W3', 'L0_cond_b3', 'L0_cond_W2', 'L0_cond_b2', 'L0_ffn_W_base', 'L0_ffn_b_base',
        'L0_ffn_A_s', 'L0_ffn_B_s', 'L0_ffn_A_r', 'L0_ffn_B_r', 'L0_ffn_W_router', 'L0_ffn_b_router']
_OUTS = [((64, 64, 512), 'float32')]


def kernel(**inputs):
    import numpy as _np
    import concourse.bacc as _bacc
    from concourse import mybir as _mybir
    from concourse.bass_utils import run_bass_kernel_spmd as _run

    nc = _bacc.Bacc("TRN2", target_bir_lowering=False, num_devices=1)
    arrays, args = {}, []
    for name in _INS:
        a = _np.ascontiguousarray(inputs[name])
        arrays[f"in_{name}_dram"] = a
        args.append(nc.dram_tensor(f"in_{name}_dram", a.shape, _mybir.dt.from_np(a.dtype), kind="ExternalInput").ap())
    for i, (shape, dtype) in enumerate(_OUTS):
        dt = _mybir.dt.from_np(_np.dtype(dtype))
        args.append(nc.dram_tensor(f"out_{i}_dram", shape, dt, kind="ExternalOutput").ap())
    adaln_ffn(nc, *args)
    r = _run(nc, [arrays], core_ids=[0])
    return r.results[0]["out_0_dram"]
```
